# Optimizing a Trainium2 kernel written in Bass

```python
import numpy as np
import jax
import jax.numpy as jnp

def _softmax(x, axis=-1):
    return jax.nn.softmax(x, axis=axis)

def _gelu(x):
    return jax.nn.gelu(x, approximate=True)

def _silu(x):
    return jax.nn.silu(x)

def _sigmoid(x):
    return jax.nn.sigmoid(x)

def _layernorm(x, axis=-1, eps=1e-05):
    m = jnp.mean(x, axis=axis, keepdims=True)
    v = jnp.var(x, axis=axis, keepdims=True)
    return (x - m) / jnp.sqrt(v + eps)

def _scatter_add(tgt, idx, src, axis=0):
    return tgt.at[idx].add(src)

def _segment_sum(src, seg, n):
    return jax.ops.segment_sum(src, seg, n)
kernel_name = 'mk_dlrm_tower_d1_rec_r8_15338d'

def setup_inputs(seed: int=0):
    np.random.seed(seed)
    _w = jnp.asarray

    def _rec_inputs():
        import jax
        import jax.numpy as jnp
        _tk = jax.random.key(seed)
        dense_ctx = jax.random.normal(jax.random.fold_in(_tk, 190), (512, 16), jnp.float32)
        ids = jnp.stack([jax.random.randint(jax.random.fold_in(_tk, 200 + f), (512,), 0, v, jnp.int32) for f, v in enumerate([1000, 1000, 1250, 125000, 1000, 1000, 1250, 12500, 125000, 125000, 12500, 1250, 12500, 12500, 1250, 12500, 12500, 125000, 1250, 1000, 1000, 12500, 1000, 1000, 12500, 125000, 1250, 12500, 125000, 125000, 1000, 1250, 1000, 1250, 1250, 12500, 1000, 1000, 12500, 1000])], axis=1)
        tbl_0 = 0.05 * jax.random.normal(jax.random.fold_in(_tk, 500 + 0), (1000, 16), jnp.float32)
        tbl_1 = 0.05 * jax.random.normal(jax.random.fold_in(_tk, 500 + 1), (1000, 16), jnp.float32)
        tbl_2 = 0.05 * jax.random.normal(jax.random.fold_in(_tk, 500 + 2), (1250, 16), jnp.float32)
        tbl_3 = 0.05 * jax.random.normal(jax.random.fold_in(_tk, 500 + 3), (125000, 16), jnp.float32)
        tbl_4 = 0.05 * jax.random.normal(jax.random.fold_in(_tk, 500 + 4), (1000, 16), jnp.float32)
        tbl_5 = 0.05 * jax.random.normal(jax.random.fold_in(_tk, 500 + 5), (1000, 16), jnp.float32)
        tbl_6 = 0.05 * jax.random.normal(jax.random.fold_in(_tk, 500 + 6), (1250, 16), jnp.float32)
        tbl_7 = 0.05 * jax.random.normal(jax.random.fold_in(_tk, 500 + 7), (12500, 16), jnp.float32)
        tbl_8 = 0.05 * jax.random.normal(jax.random.fold_in(_tk, 500 + 8), (125000, 16), jnp.float32)
        tbl_9 = 0.05 * jax.random.normal(jax.random.fold_in(_tk, 500 + 9), (125000, 16), jnp.float32)
        tbl_10 = 0.05 * jax.random.normal(jax.random.fold_in(_tk, 500 + 10), (12500, 16), jnp.float32)
        tbl_11 = 0.05 * jax.random.normal(jax.random.fold_in(_tk, 500 + 11), (1250, 16), jnp.float32)
        tbl_12 = 0.05 * jax.random.normal(jax.random.fold_in(_tk, 500 + 12), (12500, 16), jnp.float32)
        tbl_13 = 0.05 * jax.random.normal(jax.random.fold_in(_tk, 500 + 13), (12500, 16), jnp.float32)
        tbl_14 = 0.05 * jax.random.normal(jax.random.fold_in(_tk, 500 + 14), (1250, 16), jnp.float32)
        tbl_15 = 0.05 * jax.random.normal(jax.random.fold_in(_tk, 500 + 15), (12500, 16), jnp.float32)
        tbl_16 = 0.05 * jax.random.normal(jax.random.fold_in(_tk, 500 + 16), (12500, 16), jnp.float32)
        tbl_17 = 0.05 * jax.random.normal(jax.random.fold_in(_tk, 500 + 17), (125000, 16), jnp.float32)
        tbl_18 = 0.05 * jax.random.normal(jax.random.fold_in(_tk, 500 + 18), (1250, 16), jnp.float32)
        tbl_19 = 0.05 * jax.random.normal(jax.random.fold_in(_tk, 500 + 19), (1000, 16), jnp.float32)
        tbl_20 = 0.05 * jax.random.normal(jax.random.fold_in(_tk, 500 + 20), (1000, 16), jnp.float32)
        tbl_21 = 0.05 * jax.random.normal(jax.random.fold_in(_tk, 500 + 21), (12500, 16), jnp.float32)
        tbl_22 = 0.05 * jax.random.normal(jax.random.fold_in(_tk, 500 + 22), (1000, 16), jnp.float32)
        tbl_23 = 0.05 * jax.random.normal(jax.random.fold_in(_tk, 500 + 23), (1000, 16), jnp.float32)
        tbl_24 = 0.05 * jax.random.normal(jax.random.fold_in(_tk, 500 + 24), (12500, 16), jnp.float32)
        tbl_25 = 0.05 * jax.random.normal(jax.random.fold_in(_tk, 500 + 25), (125000, 16), jnp.float32)
        tbl_26 = 0.05 * jax.random.normal(jax.random.fold_in(_tk, 500 + 26), (1250, 16), jnp.float32)
        tbl_27 = 0.05 * jax.random.normal(jax.random.fold_in(_tk, 500 + 27), (12500, 16), jnp.float32)
        tbl_28 = 0.05 * jax.random.normal(jax.random.fold_in(_tk, 500 + 28), (125000, 16), jnp.float32)
        tbl_29 = 0.05 * jax.random.normal(jax.random.fold_in(_tk, 500 + 29), (125000, 16), jnp.float32)
        tbl_30 = 0.05 * jax.random.normal(jax.random.fold_in(_tk, 500 + 30), (1000, 16), jnp.float32)
        tbl_31 = 0.05 * jax.random.normal(jax.random.fold_in(_tk, 500 + 31), (1250, 16), jnp.float32)
        tbl_32 = 0.05 * jax.random.normal(jax.random.fold_in(_tk, 500 + 32), (1000, 16), jnp.float32)
        tbl_33 = 0.05 * jax.random.normal(jax.random.fold_in(_tk, 500 + 33), (1250, 16), jnp.float32)
        tbl_34 = 0.05 * jax.random.normal(jax.random.fold_in(_tk, 500 + 34), (1250, 16), jnp.float32)
        tbl_35 = 0.05 * jax.random.normal(jax.random.fold_in(_tk, 500 + 35), (12500, 16), jnp.float32)
        tbl_36 = 0.05 * jax.random.normal(jax.random.fold_in(_tk, 500 + 36), (1000, 16), jnp.float32)
        tbl_37 = 0.05 * jax.random.normal(jax.random.fold_in(_tk, 500 + 37), (1000, 16), jnp.float32)
        tbl_38 = 0.05 * jax.random.normal(jax.random.fold_in(_tk, 500 + 38), (12500, 16), jnp.float32)
        tbl_39 = 0.05 * jax.random.normal(jax.random.fold_in(_tk, 500 + 39), (1000, 16), jnp.float32)
        _rk = jax.random.fold_in(_tk, 7)
        W_top1 = 0.05 * jax.random.normal(jax.random.fold_in(_tk, 801), (400, 512), jnp.float32)
        W_top2 = 0.0441942 * jax.random.normal(jax.random.fold_in(_tk, 802), (512, 256), jnp.float32)
        W_top3 = 0.0625 * jax.random.normal(jax.random.fold_in(_tk, 803), (256, 1), jnp.float32)
        b_top1 = jnp.zeros((512,), jnp.float32)
        b_top2 = jnp.zeros((256,), jnp.float32)
        return (dense_ctx, ids, tbl_0, tbl_1, tbl_2, tbl_3, tbl_4, tbl_5, tbl_6, tbl_7, tbl_8, tbl_9, tbl_10, tbl_11, tbl_12, tbl_13, tbl_14, tbl_15, tbl_16, tbl_17, tbl_18, tbl_19, tbl_20, tbl_21, tbl_22, tbl_23, tbl_24, tbl_25, tbl_26, tbl_27, tbl_28, tbl_29, tbl_30, tbl_31, tbl_32, tbl_33, tbl_34, tbl_35, tbl_36, tbl_37, tbl_38, tbl_39, W_top1, b_top1, W_top2, b_top2, W_top3)
    dense_ctx, ids, tbl_0, tbl_1, tbl_2, tbl_3, tbl_4, tbl_5, tbl_6, tbl_7, tbl_8, tbl_9, tbl_10, tbl_11, tbl_12, tbl_13, tbl_14, tbl_15, tbl_16, tbl_17, tbl_18, tbl_19, tbl_20, tbl_21, tbl_22, tbl_23, tbl_24, tbl_25, tbl_26, tbl_27, tbl_28, tbl_29, tbl_30, tbl_31, tbl_32, tbl_33, tbl_34, tbl_35, tbl_36, tbl_37, tbl_38, tbl_39, W_top1, b_top1, W_top2, b_top2, W_top3 = _rec_inputs()

    def _L0_rec_setup():
        import jax, jax.numpy as jnp
        import numpy as np
        B, M, D = (512, 40, 16)
        DIMS = [128, 128, 128]
        key = jax.random.key(seed)
        k_x, k0, k1, k2 = jax.random.split(key, 4)
        scale = lambda fan_in: (2.0 / fan_in) ** 0.5
        x0 = jax.random.normal(k_x, (B, M, D), dtype=jnp.float32)
        kern0 = jax.random.normal(k0, (DIMS[0], M, M), dtype=jnp.float32) * scale(M * M)
        kern1 = jax.random.normal(k1, (DIMS[1], DIMS[0], M), dtype=jnp.float32) * scale(DIMS[0] * M)
        kern2 = jax.random.normal(k2, (DIMS[2], DIMS[1], M), dtype=jnp.float32) * scale(DIMS[1] * M)
        return {'x0': x0, 'k0': kern0, 'k1': kern1, 'k2': kern2}
    _L0_rec_all = _L0_rec_setup()
    _L0_rec_in = {k: v for k, v in _L0_rec_all.items() if k in ('k0', 'k1', 'k2')}
    del _L0_rec_all
    return {'dense_ctx': dense_ctx, 'ids': ids, 'tbl_0': tbl_0, 'tbl_1': tbl_1, 'tbl_2': tbl_2, 'tbl_3': tbl_3, 'tbl_4': tbl_4, 'tbl_5': tbl_5, 'tbl_6': tbl_6, 'tbl_7': tbl_7, 'tbl_8': tbl_8, 'tbl_9': tbl_9, 'tbl_10': tbl_10, 'tbl_11': tbl_11, 'tbl_12': tbl_12, 'tbl_13': tbl_13, 'tbl_14': tbl_14, 'tbl_15': tbl_15, 'tbl_16': tbl_16, 'tbl_17': tbl_17, 'tbl_18': tbl_18, 'tbl_19': tbl_19, 'tbl_20': tbl_20, 'tbl_21': tbl_21, 'tbl_22': tbl_22, 'tbl_23': tbl_23, 'tbl_24': tbl_24, 'tbl_25': tbl_25, 'tbl_26': tbl_26, 'tbl_27': tbl_27, 'tbl_28': tbl_28, 'tbl_29': tbl_29, 'tbl_30': tbl_30, 'tbl_31': tbl_31, 'tbl_32': tbl_32, 'tbl_33': tbl_33, 'tbl_34': tbl_34, 'tbl_35': tbl_35, 'tbl_36': tbl_36, 'tbl_37': tbl_37, 'tbl_38': tbl_38, 'tbl_39': tbl_39, 'W_top1': W_top1, 'b_top1': b_top1, 'W_top2': W_top2, 'b_top2': b_top2, 'W_top3': W_top3, 'L0_rec_k0': _L0_rec_in['k0'], 'L0_rec_k1': _L0_rec_in['k1'], 'L0_rec_k2': _L0_rec_in['k2']}

def reference(dense_ctx, ids, tbl_0, tbl_1, tbl_2, tbl_3, tbl_4, tbl_5, tbl_6, tbl_7, tbl_8, tbl_9, tbl_10, tbl_11, tbl_12, tbl_13, tbl_14, tbl_15, tbl_16, tbl_17, tbl_18, tbl_19, tbl_20, tbl_21, tbl_22, tbl_23, tbl_24, tbl_25, tbl_26, tbl_27, tbl_28, tbl_29, tbl_30, tbl_31, tbl_32, tbl_33, tbl_34, tbl_35, tbl_36, tbl_37, tbl_38, tbl_39, W_top1, b_top1, W_top2, b_top2, W_top3, L0_rec_k0, L0_rec_k1, L0_rec_k2):
    import jax
    import jax.numpy as jnp

    def _L0_rec_ref(x0, k0, k1, k2):
        import jax, jax.numpy as jnp
        import numpy as np
        B, M, D = (512, 40, 16)
        DIMS = [128, 128, 128]
        x = x0
        outputs = []
        for k in (k0, k1, k2):
            x = jnp.einsum('bhd,bmd,ohm->bod', x, x0, k)
            outputs.append(jnp.sum(x, axis=-1))
        return jnp.concatenate(outputs, axis=1)
    e = jnp.stack([tbl_0[ids[:, 0]], tbl_1[ids[:, 1]], tbl_2[ids[:, 2]], tbl_3[ids[:, 3]], tbl_4[ids[:, 4]], tbl_5[ids[:, 5]], tbl_6[ids[:, 6]], tbl_7[ids[:, 7]], tbl_8[ids[:, 8]], tbl_9[ids[:, 9]], tbl_10[ids[:, 10]], tbl_11[ids[:, 11]], tbl_12[ids[:, 12]], tbl_13[ids[:, 13]], tbl_14[ids[:, 14]], tbl_15[ids[:, 15]], tbl_16[ids[:, 16]], tbl_17[ids[:, 17]], tbl_18[ids[:, 18]], tbl_19[ids[:, 19]], tbl_20[ids[:, 20]], tbl_21[ids[:, 21]], tbl_22[ids[:, 22]], tbl_23[ids[:, 23]], tbl_24[ids[:, 24]], tbl_25[ids[:, 25]], tbl_26[ids[:, 26]], tbl_27[ids[:, 27]], tbl_28[ids[:, 28]], tbl_29[ids[:, 29]], tbl_30[ids[:, 30]], tbl_31[ids[:, 31]], tbl_32[ids[:, 32]], tbl_33[ids[:, 33]], tbl_34[ids[:, 34]], tbl_35[ids[:, 35]], tbl_36[ids[:, 36]], tbl_37[ids[:, 37]], tbl_38[ids[:, 38]], tbl_39[ids[:, 39]]], axis=1)
    z = _L0_rec_ref(e, L0_rec_k0, L0_rec_k1, L0_rec_k2)
    z = z.reshape(z.shape[0], -1)
    h = jnp.concatenate([z, dense_ctx], axis=1)
    h = jnp.maximum(h @ W_top1 + b_top1, 0.0)
    h = jnp.maximum(h @ W_top2 + b_top2, 0.0)
    y = h @ W_top3
    return y

_drawn_inputs = setup_inputs


def setup_inputs(seed=0):
    import zlib

    import numpy as np

    out = dict(_drawn_inputs(seed))
    spreads = {'b_top1': (0.0, 0.532), 'b_top2': (0.0, 0.1)}
    factors = {'tbl_0': 7.49,
     'tbl_1': 7.131,
     'tbl_2': 6.499,
     'tbl_3': 7.137,
     'tbl_4': 7.168,
     'tbl_5': 7.37,
     'tbl_6': 6.788,
     'tbl_7': 7.427,
     'tbl_8': 6.676,
     'tbl_9': 7.128,
     'tbl_10': 7.101,
     'tbl_11': 6.913,
     'tbl_12': 6.737,
     'tbl_13': 6.873,
     'tbl_14': 6.499,
     'tbl_15': 7.331,
     'tbl_16': 7.245,
     'tbl_17': 6.556,
     'tbl_18': 7.423,
     'tbl_19': 6.637,
     'tbl_20': 7.013,
     'tbl_21': 7.011,
     'tbl_22': 7.322,
     'tbl_23': 6.806,
     'tbl_24': 7.017,
     'tbl_25': 6.57,
     'tbl_26': 6.586,
     'tbl_27': 6.668,
     'tbl_28': 6.192,
     'tbl_29': 7.822,
     'tbl_30': 6.886,
     'tbl_31': 7.16,
     'tbl_32': 6.784,
     'tbl_33': 6.059,
     'tbl_34': 7.46,
     'tbl_35': 6.395,
     'tbl_36': 6.718,
     'tbl_37': 6.419,
     'tbl_38': 6.716,
     'tbl_39': 6.282,
     'L0_rec_k1': 8.0,
     'L0_rec_k2': 8.0}
    for name, (base, spread) in spreads.items():
        noise = np.random.default_rng([zlib.crc32(name.encode()), seed]).standard_normal(out[name].shape)
        drawn = base * np.exp(spread * noise) if base else spread * noise
        out[name] = jnp.asarray(drawn.astype(out[name].dtype))
    for name, factor in factors.items():
        out[name] = (out[name] * factor).astype(out[name].dtype)
    return out
```

```python
import concourse.bass as bass
from concourse import mybir
from contextlib import ExitStack



def cin_tower(nc, dense_ctx, ids, tables, W_top1, b_top1, W_top2, b_top2, W_top3, k0, k1, k2, out):
    fp32 = mybir.dt.float32
    fp32r = mybir.dt.float32r
    i32 = mybir.dt.int32
    u32 = mybir.dt.uint32
    ALU = mybir.AluOpType
    ACT = mybir.ActivationFunctionType
    AX = mybir.AxisListType

    B, M = ids.shape
    D = tables[0].shape[1]
    H = k1.shape[0]
    P = 128
    NBT = B // P
    CB = 32
    CW = CB * D
    NC = B // CB
    TB = P // D
    KT = CW // P
    NT = NC * KT
    SH = 3
    PB = SH * M
    NJ = (M // 2 + 1) // SH
    NS = NJ * SH
    UM = CW // H
    NQ = M // UM
    M1 = M + 1
    DG = 4
    NG = D // DG
    N1, N2 = W_top1.shape[1], W_top2.shape[1]
    J1, J2 = N1 // P, N2 // P
    ND = dense_ctx.shape[1]

    WHO = "VAVAVVAVAV"
    V_UNITS = [q for q in range(NQ) if WHO[q] == "V"]
    A_UNITS = [q for q in range(NQ) if WHO[q] == "A"]
    NV, NA = len(V_UNITS), len(A_UNITS)
    VS = NV * UM
    GA = NA + 1
    NY = 4
    NP = 2

    U_PREP = [0, 1, 5, 6]
    U_PREP_LATE = [32, 33, 36, 38]
    U_BASE, U_BASED = 7, 8
    U_SHIFT = [9, 13, 16, 19, 21, 24, 27]
    U_X0T, U_X0TED = 12, 13
    U_PROD = [u + 1 for u in U_SHIFT]
    U_FOLD = [u + 5 for u in U_SHIFT]
    U_X1H, U_X1L, U_Z1 = 34, 36, 37
    Q_SUM, Q_G, Q_GOUT = 5, 8, 9

    ctx = ExitStack()
    with ctx:
        def sb(name, shape, dt=fp32):
            return ctx.enter_context(nc.sbuf_tensor(name, shape, dt))

        def sem(name):
            return ctx.enter_context(nc.semaphore(name))

        region = sb("region", [P, M1 * B])
        G = region[:, :].rearrange("p (m b) -> p m b", m=M1)
        at = [0]

        def carve(n):
            at[0] += n
            assert at[0] <= M1 * B
            return region[:, at[0] - n:at[0]]
        k0_raw = carve(M * M)
        k1_raw = carve(H * M)
        k2_raw = carve(H * M)
        w0_pre = carve(NS * M)
        sel_f = carve((1 + NJ) * PB)[0:2 * M, :]

        k1_hi = sb("k1_hi", [P, M * H], fp32r)
        k1_lo = sb("k1_lo", [P, M * H], fp32r)
        k2_t = sb("k2_t", [P, M * H])
        w0_t = sb("w0_t", [PB, NJ * H])
        sel = sb("sel", [2 * M, (1 + NJ) * PB], fp32r)
        ident = sb("ident", [P, P])
        row_mask = sb("row_mask", [P, TB])
        idx = sb("idx", [P, NBT * M], i32)
        emb = sb("emb", [P, M * NBT * D])
        halves = sb("halves", [P, DG * 2 * M])
        xs = sb("xs", [2 * M, 2 * P * D], fp32r)
        base = sb("base", [PB, CW])
        prod = sb("prod", [P, NP * CW])
        x0t = sb("x0t", [P, 2 * KT * M1])
        x0c = sb("x0c", [P, 2 * M1])
        x1_hi = sb("x1_hi", [P, CW], fp32r)
        x1_lo = sb("x1_lo", [P, CW], fp32r)
        acc = sb("acc", [P, 2 * 2 * H])
        x2t = sb("x2t", [P, 2 * H])
        zw = sb("zw", [P, NA * CW])
        psum4 = sb("psum4", [P, CW])
        pacc = sb("pacc", [P, 2 * H])
        diag = sb("diag", [P, TB * M1])
        z1 = sb("z1", [P, B])
        rows = sb("rows", [J1 + 2 * J2, P])
        cols = sb("cols", [P, J1 + 2 * J2])
        b1c, b2c, w3c = cols[:, 0:J1], cols[:, J1:J1 + J2], cols[:, J1 + J2:]
        dense = sb("dense", [P, NBT * ND])
        dense_t = base[0:ND, 0:B]
        w1 = zw[:, 0:3 * N1]
        w1d = psum4[0:ND, 0:N1]
        h1 = emb[:, 0:J1 * B]
        z3 = prod[:, 0:B]
        h2 = k2_t[:, 0:J2 * B]
        w2 = k2_t[:, J2 * B:J2 * B + J1 * N2]
        y_row = acc[0:1, 0:B]

        y_bank = [ctx.enter_context(nc.psum_tensor(f"y_bank{i}", [P, CW], fp32)) for i in range(NY)]
        ring = [ctx.enter_context(nc.psum_tensor(f"ring{i}", [P, CW], fp32)) for i in range(2)]
        x_bank = ctx.enter_context(nc.psum_tensor("x_bank", [P, CW], fp32))
        g_bank = ctx.enter_context(nc.psum_tensor("g_bank", [P, CW], fp32))

        ids_in = sem("ids_in")
        k0_in, k1_in, k2_in = sem("k0_in"), sem("k1_in"), sem("k2_in")
        small_in = sem("small_in")
        w_in, w2_in = sem("w_in"), sem("w2_in")
        gathered = sem("gathered")
        consts = sem("consts")
        const_step = sem("const_step")
        sel_ready = sem("sel_ready")
        w0_step, w0_ready = sem("w0_step"), sem("w0_ready")
        turned_k = sem("turned_k")
        act_setup, dve_setup = sem("act_setup"), sem("dve_setup")
        split_hi, split_lo = sem("split_hi"), sem("split_lo")
        turned, turn_out = sem("turned"), sem("turn_out")
        based, base_out = sem("based"), sem("base_out")
        shifted, prod_done = sem("shifted"), sem("prod_done")
        x0_turned, x0t_out = sem("x0_turned"), sem("x0t_out")
        folded = sem("folded")
        x1h_done, x1l_done, z1_done = sem("x1h_done"), sem("x1l_done"), sem("z1_done")
        y_ready = sem("y_ready")
        v_step, a_unit, p_add = sem("v_step"), sem("a_unit"), sem("p_add")
        x0c_ready, diag_ready = sem("x0c_ready"), sem("diag_ready")
        sum_half, x2_ready = sem("sum_half"), sem("x2_ready")
        g_done, g_out = sem("g_done"), sem("g_out")
        z3_done, z3_out = sem("z3_done"), sem("z3_out")
        dense_done, dense_out = sem("dense_done"), sem("dense_out")
        h1_done, h1_act, h1_dve = sem("h1_done"), sem("h1_act"), sem("h1_dve")
        h2_done, h2_act, h2_dve = sem("h2_done"), sem("h2_act"), sem("h2_dve")
        y_done, y_copied, y_stored = sem("y_done"), sem("y_copied"), sem("y_stored")

        def wait(eng, s, n):
            if isinstance(n, int) and n <= 0:
                return
            eng.wait_ge(s, n)

        def freed_by(q, t):
            if q in V_UNITS:
                return v_step, t * VS + UM * (V_UNITS.index(q) + 1)
            return a_unit, t * NA + A_UNITS.index(q) + 1

        GROUPS = [("k0", g) for g in range(-(-NJ // 4))] + [("k1", g) for g in range(NQ)] + \
                 [("k2", g) for g in range(NQ)]
        G_K1 = [i for i, g in enumerate(GROUPS) if g[0] == "k1"]
        G_ACT = [i for i, g in enumerate(GROUPS) if g[0] != "k1" or True]

        def emb_step(n):
            return emb[:, :].rearrange("p (f r) -> p f r", f=M)[:, :, bass.ds(n * DG, DG)]

        SHIFT_BANK = [0, 0, 1, 0, 1, 0, 1]

        def prod_slot(j):
            return j % NP

        h1_bank = [y_bank[1], y_bank[2], y_bank[3], x_bank]
        h2_bank = [ring[0], ring[1]]
        def prep_at(c, step):
            return (U_PREP_LATE if isinstance(c, int) and c == 0 else U_PREP)[step]

        halves_v = halves[:, :].rearrange("p (d s f) -> p d s f", d=DG, s=2)

        block = ctx.enter_context(nc.Block())

        @block.sync
        def _(sp):
            sp.dma_start(idx[:, :].rearrange("p (t f) -> p t f", t=NBT),
                         ids.rearrange("(t p) f -> p t f", p=P)).then_inc(ids_in, 16)
            sp.dma_start(k0_raw, k0.rearrange("o h m -> o (h m)")).then_inc(k0_in, 16)
            sp.dma_start(k1_raw, k1.rearrange("o h m -> o (h m)")).then_inc(k1_in, 16)
            sp.dma_start(k2_raw, k2.rearrange("o h m -> o (h m)")).then_inc(k2_in, 16)
            sp.dma_start(rows[0:J1, :], b_top1.rearrange("(j p) -> j p", p=P)).then_inc(small_in, 16)
            sp.dma_start(rows[J1:J1 + J2, :], b_top2.rearrange("(j p) -> j p", p=P)).then_inc(small_in, 16)
            sp.dma_start(rows[J1 + J2:J1 + 2 * J2, :],
                         W_top3.rearrange("(j p) n -> j (p n)", p=P)).then_inc(small_in, 16)
            sp.dma_start(dense[:, :].rearrange("p (t n) -> p t n", t=NBT),
                         dense_ctx.rearrange("(t p) n -> p t n", p=P)).then_inc(small_in, 16)
            sp.wait_ge(p_add, NT * GA)
            sp.dma_start(w1.rearrange("p (j n) -> p j n", j=3),
                         W_top1[0:3 * H, :].rearrange("(j p) n -> p j n", p=P)).then_inc(w_in, 16)
            sp.dma_start(w1d, W_top1[3 * H:3 * H + ND, :]).then_inc(w_in, 16)
            sp.wait_ge(z3_done, 1)
            sp.dma_start(w2.rearrange("p (j n) -> p j n", j=J1),
                         W_top2.rearrange("(j p) n -> p j n", p=P)).then_inc(w2_in, 16)
            sp.wait_ge(y_copied, 1)
            sp.dma_start(out.rearrange("b n -> n b"), y_row).then_inc(y_stored, 16)
            sp.wait_ge(y_stored, 16)

        @block.gpsimd
        def _(pool):
            pool.memset(ident[:, :], 0.0).then_inc(const_step, 1)
            pool.wait_ge(const_step, 1)
            pool.affine_select(out=ident[:, :], in_=ident[:, :], compare_op=ALU.not_equal, fill=1.0,
                               base=0, pattern=[[-1, P]], channel_multiplier=1).then_inc(consts, 1)

            def gather(t, features):
                if 0 in features:
                    wait(pool, gathered, 16 * M * t)
                for f in features:
                    a = (f * NBT + t) * D
                    pool.indirect_dma_start(
                        out=emb[:, a:a + D], out_offset=None, in_=tables[f],
                        in_offset=bass.IndirectOffsetOnAxis(
                            ap=idx[:, t * M + f:t * M + f + 1].bitcast(u32), axis=0),
                    ).then_inc(gathered, 16)

            pool.wait_ge(ids_in, 16)
            gather(0, range(M))

            pool.memset(sel_f, 0.0).then_inc(const_step, 1)
            steps = 2
            for w in (0, 1):
                v = sel_f[:, 0:PB].rearrange("p (r i) -> p r i", r=SH)
                pool.wait_ge(const_step, steps)
                pool.affine_select(out=v, in_=v, compare_op=ALU.not_equal, fill=1.0, base=-M * w,
                                   pattern=[[0, SH], [-1, M]], channel_multiplier=1).then_inc(const_step, 1)
                steps += 1
            for w in (-1, 0, 1):
                v = sel_f[:, PB:].rearrange("p (j r i) -> p j r i", j=NJ, r=SH)
                pool.wait_ge(const_step, steps)
                pool.affine_select(out=v, in_=v, compare_op=ALU.not_equal, fill=1.0, base=-M * w,
                                   pattern=[[-SH, NJ], [-1, SH], [-1, M]],
                                   channel_multiplier=1).then_inc(const_step, 1)
                steps += 1
            pool.memset(row_mask[:, :], 1.0).then_inc(const_step, 1)
            steps += 1
            pool.wait_ge(const_step, steps)
            pool.affine_select(out=row_mask[:, :], in_=row_mask[:, :], compare_op=ALU.is_ge, fill=0.0,
                               base=0, pattern=[[-D, TB]], channel_multiplier=1).then_inc(const_step, 1)
            steps += 1
            pool.wait_ge(const_step, steps)
            pool.affine_select(out=row_mask[:, :], in_=row_mask[:, :], compare_op=ALU.is_ge, fill=0.0,
                               base=D - 1, pattern=[[D, TB]], channel_multiplier=-1).then_inc(const_step, 1)
            steps += 1
            pool.memset(x0t[:, :], 1.0).then_inc(const_step, 1)
            steps += 1
            pool.wait_ge(const_step, steps)
            pool.engine_nop().then_inc(consts, 1)

            gather(1, range(M))

            def load_x0c(t, k):
                c = t if isinstance(t, int) else t
                return c

            def next_x0c(c, k):
                t = c * KT + k + 1
                if k == KT - 1:
                    cc, kk = c + 1, 0
                else:
                    cc, kk = c, k + 1
                wait(pool, x0t_out, cc + 1)
                wait(pool, v_step, (t - 1) * VS)
                wait(pool, a_unit, (t - 1) * NA)
                wait(pool, diag_ready, t - 1)
                par = (k + 1) % 2
                pool.tensor_copy(x0c[:, par * M1:(par + 1) * M1],
                                 x0t[:, bass.ds((cc % 2) * (KT * M1) + kk * M1, M1)]).then_inc(x0c_ready, 1)

            def diagonal(c, k):
                t = c * KT + k
                wait(pool, x0c_ready, t + 1)
                wait(pool, g_done, t)
                par = k % 2
                shape = [P, TB, M1]
                pool.tensor_tensor(
                    diag[:, :].rearrange("p (b m) -> p b m", b=TB),
                    x0c[:, par * M1:(par + 1) * M1].unsqueeze(1).broadcast_to(shape),
                    row_mask[:, :].unsqueeze(2).broadcast_to(shape), ALU.mult).then_inc(diag_ready, 1)

            def add_units(c, k):
                t = c * KT + k
                for a in range(1, NA):
                    pool.wait_ge(a_unit, t * NA + a + 1)
                    if a == 1:
                        one = zw[:, 0:CW]
                        wait(pool, p_add, t * GA)
                    else:
                        one = psum4[:, :]
                        pool.wait_ge(p_add, t * GA + a - 1)
                    pool.tensor_tensor(psum4[:, :], one, zw[:, a * CW:(a + 1) * CW], ALU.add).then_inc(p_add, 1)
                pool.wait_ge(p_add, t * GA + NA - 1)
                pool.tensor_tensor(psum4[:, 0:CW // 2], psum4[:, 0:CW // 2], psum4[:, CW // 2:CW], ALU.add).then_inc(p_add, 1)
                pool.wait_ge(p_add, t * GA + NA)
                wait(pool, x2_ready, t - 1)
                par = k % 2
                pool.tensor_tensor(pacc[:, par * H:(par + 1) * H], psum4[:, 0:H], psum4[:, H:2 * H],
                                   ALU.add).then_inc(p_add, 1)

            def chunk(c, last, gathers=()):
                g = 0
                for k in range(KT):
                    if not (last and k == KT - 1):
                        if k > 0 or True:
                            next_x0c(c, k)
                    for part in gathers[k:k + 1]:
                        gather(*part)
                    add_units(c, k)
                    diagonal(c, k)

            pool.wait_ge(x0t_out, 1)
            pool.tensor_copy(x0c[:, 0:M1], x0t[:, 0:M1]).then_inc(x0c_ready, 1)
            GC = 4
            FG = -(-M // (GC * KT))
            for c in range(2 * GC):
                t = 2 + c // GC
                first = (c % GC) * KT * FG
                chunk(c, False, [(t, range(min(M, first + FG * k), min(M, first + FG * (k + 1))))
                                 for k in range(KT)])
            with pool.Fori(2 * GC, NC - 1) as c:
                chunk(c, False)
            chunk(NC - 1, True)

        @block.scalar
        def _(act):
            def setup_out(i):
                kind, g = GROUPS[i]
                act.wait_ge(turned_k, i + 1)
                src = y_bank[i % NY]
                if kind == "k0":
                    n = min(4, NJ - 4 * g) * H
                    act.activation(w0_t[:, 4 * g * H:4 * g * H + n], src[0:PB, 0:n], ACT.Copy).then_inc(act_setup, 1)
                elif kind == "k1":
                    act.activation(k1_hi[:, g * CW:(g + 1) * CW], src[:, :], ACT.Copy).then_inc(act_setup, 1)
                else:
                    act.activation(k2_t[:, g * CW:(g + 1) * CW], src[:, :], ACT.Copy).then_inc(act_setup, 1)

            def split(n):
                act.wait_ge(gathered, (n // NG + 1) * (16 * M))
                wait(act, turned, n)
                act.activation(halves_v[:, :, 0, :].bitcast(fp32r), emb_step(n).rearrange("p f d -> p d f"),
                               ACT.Copy).then_inc(split_hi, 1)

            def turn_evac(n, c):
                act.wait_ge(turned, n + 1)
                wait(act, shifted, c * NJ)
                v = xs[:, :].rearrange("p (r b g e) -> p r g b e", r=2, b=P, g=NG)
                act.activation(v[:, (n // NG) % 2, n % NG, :, :],
                               ring[0][0:2 * M, :].rearrange("p (e b) -> p b e", e=DG),
                               ACT.Copy).then_inc(turn_out, 1)

            def base_evac(c):
                act.wait_ge(based, c + 1)
                wait(act, prod_done, c * NJ)
                wait(act, x0_turned, c)
                act.activation(base[:, :], ring[1][0:PB, :], ACT.Copy).then_inc(base_out, 1)

            def x1_hi_out(c, k0_, k1_):
                act.wait_ge(folded, NJ * (c + 1))
                wait(act, y_ready, ((c - 1) * KT + k1_) * NQ)
                if k0_:
                    act.wait_ge(x1l_done, 2 * c + 1)
                    act.wait_ge(z1_done, c + 1)
                s = slice(k0_ * P, k1_ * P)
                act.activation(x1_hi[:, s], x_bank[:, s], ACT.Copy).then_inc(x1h_done, 1)

            def weigh(c, k, q):
                t = c * KT + k
                a = A_UNITS.index(q)
                act.wait_ge(y_ready, t * NQ + q + 1)
                if a == 0:
                    act.wait_ge(x0c_ready, t + 1)
                wait(act, p_add, (t - 1) * GA + max(a, 1))
                par = k % 2
                for i in range(UM):
                    m = q * UM + i
                    last = act.activation(zw[:, a * CW + i * H:a * CW + (i + 1) * H],
                                          y_bank[(k * NQ + q) % NY][:, i * H:(i + 1) * H], ACT.Copy,
                                          scale=x0c[:, par * M1 + m:par * M1 + m + 1])
                last.then_inc(a_unit, 1)

            def g_evac(t):
                act.wait_ge(g_done, t + 1)
                act.activation(G[:, :, bass.ds(t * TB, TB)],
                               g_bank[:, 0:TB * M1].rearrange("p (b m) -> p m b", b=TB),
                               ACT.Copy).then_inc(g_out, 1)

            def chunk(c, prep, layer1):
                for u in range(KT * NQ):
                    k, q = divmod(u, NQ)
                    if prep and u == prep_at(c, 0):
                        split(c + NG)
                    if prep and u == prep_at(c, 3):
                        turn_evac(c + NG, c + 1)
                    if layer1 and u == U_BASED:
                        base_evac(c + 1)
                    if q == Q_GOUT and not (k == 0 and isinstance(c, int) and c == 0):
                        g_evac(c * KT + k - 1)
                    if WHO[q] == "A":
                        weigh(c, k, q)
                    if layer1 and u == U_X1H:
                        x1_hi_out(c + 1, 0, KT - 1)
                if layer1:
                    x1_hi_out(c + 1, KT - 1, KT)

            for i in range(len(GROUPS)):
                setup_out(i)
            for n in range(NG):
                split(n)
                turn_evac(n, 0)
            base_evac(0)
            x1_hi_out(0, 0, KT - 1)
            x1_hi_out(0, KT - 1, KT)
            chunk(0, True, True)
            with act.Fori(1, NC - NG) as c:
                chunk(c, True, True)
            with act.Fori(NC - NG, NC - 1) as c:
                chunk(c, False, True)
            chunk(NC - 1, False, False)
            g_evac(NT - 1)
            act.wait_ge(small_in, 64)
            act.wait_ge(dense_done, 1)
            act.activation(dense_t, ring[0][0:ND, 0:B], ACT.Copy).then_inc(dense_out, 1)
            act.activation(cols[:, :], ring[1][:, 0:J1 + 2 * J2], ACT.Copy).then_inc(dense_out, 1)
            act.wait_ge(dense_out, 2)
            act.wait_ge(z3_done, 1)
            act.activation(z3, y_bank[0][:, :], ACT.Copy).then_inc(z3_out, 1)
            for j in range(0, J1, 2):
                act.wait_ge(h1_done, j + 1)
                act.activation(h1[:, j * B:(j + 1) * B], h1_bank[j][:, :], ACT.Relu,
                               bias=b1c[:, j:j + 1]).then_inc(h1_act, 1)
            act.wait_ge(h2_done, 1)
            act.activation(h2[:, 0:B], h2_bank[0][:, :], ACT.Relu, bias=b2c[:, 0:1]).then_inc(h2_act, 1)

        @block.vector
        def _(dve):
            dve.wait_ge(k0_in, 16)
            for s in range(NS):
                for lo, hi, wrap in ((0, M - s, 0), (M - s, M, 1)):
                    if lo == hi:
                        continue
                    n = hi - lo
                    a = lo * (M + 1) + s - wrap * M
                    b = lo * (M + 1) + s * M - wrap * M * M
                    dst = w0_pre[:, s * M + lo:s * M + hi]
                    one = k0_raw[:, a:a + (n - 1) * (M + 1) + 1:M + 1]
                    two = k0_raw[:, b:b + (n - 1) * (M + 1) + 1:M + 1]
                    if s == 0 or 2 * s == M:
                        last = dve.tensor_copy(dst, one)
                    else:
                        last = dve.tensor_tensor(dst, one, two, ALU.add)
                    last.then_inc(w0_ready, 1)
            W0_OPS = 2 * NS - 1
            dve.wait_ge(consts, 2)
            dve.tensor_copy(sel[:, :], sel_f).then_inc(sel_ready, 1)
            for i in G_K1:
                g = GROUPS[i][1]
                dve.wait_ge(act_setup, i + 1)
                s = slice(g * CW, (g + 1) * CW)
                dve.tensor_tensor(k1_lo[:, s], y_bank[i % NY][:, :], k1_hi[:, s].bitcast(fp32),
                                  ALU.subtract).then_inc(dve_setup, 1)

            def split(n):
                dve.wait_ge(split_hi, n + 1)
                dve.tensor_tensor(halves_v[:, :, 1, :], emb_step(n).rearrange("p f d -> p d f"),
                                  halves_v[:, :, 0, :], ALU.subtract).then_inc(split_lo, 1)

            def product(c, j):
                if j == 0:
                    dve.wait_ge(base_out, c + 1)
                dve.wait_ge(shifted, c * NJ + j + 1)
                wait(dve, folded, c * NJ + j - NP + 1)
                b = prod_slot(j)
                dve.tensor_tensor(prod[0:PB, b * CW:(b + 1) * CW], base[:, :], ring[SHIFT_BANK[j]][0:PB, :],
                                  ALU.mult).then_inc(prod_done, 1)

            def x0t_evac(c):
                dve.wait_ge(x0_turned, c + 1)
                wait(dve, x0c_ready, (c - 1) * KT)
                if isinstance(c, int) and c == 0:
                    dve.wait_ge(consts, 2)
                v = x0t[:, :].rearrange("p (c k m) -> p c k m", c=2, k=KT)
                dve.tensor_copy(v[:, c % 2, :, 0:M],
                                ring[1][:, 0:KT * PB].rearrange("p (k m) -> p k m", k=KT)[:, :, 0:M]).then_inc(x0t_out, 1)

            def x1_lo_out(c, k0_, k1_, n):
                dve.wait_ge(x1h_done, 2 * c + n)
                s = slice(k0_ * P, k1_ * P)
                dve.tensor_tensor(x1_lo[:, s], x_bank[:, s], x1_hi[:, s].bitcast(fp32),
                                  ALU.subtract).then_inc(x1l_done, 1)

            def z1_out(c):
                dve.tensor_reduce(z1[:, bass.ds(c * CB, CB)], x_bank[:, :].rearrange("p (b d) -> p b d", b=CB),
                                  AX.X, ALU.add).then_inc(z1_done, 1)

            def weigh(c, k, q):
                t = c * KT + k
                v = V_UNITS.index(q)
                par = k % 2
                dve.wait_ge(y_ready, t * NQ + q + 1)
                if v == 0:
                    dve.wait_ge(x0c_ready, t + 1)
                    wait(dve, x2_ready, t - 1)
                for i in range(UM):
                    n = v * UM + i
                    m = q * UM + i
                    a = acc[:, (2 * par + n % 2) * H:(2 * par + n % 2 + 1) * H]
                    y = y_bank[(k * NQ + q) % NY][:, i * H:(i + 1) * H]
                    e = x0c[:, par * M1 + m:par * M1 + m + 1]
                    if n < 2:
                        dve.tensor_scalar(a, y, e, None, ALU.mult).then_inc(v_step, 1)
                    else:
                        dve.wait_ge(v_step, t * VS + n - 1)
                        dve.scalar_tensor_tensor(out=a, in0=y, scalar=e, in1=a, op0=ALU.mult,
                                                 op1=ALU.add).then_inc(v_step, 1)

            def sum_tile(t, k):
                par = k % 2
                dve.wait_ge(v_step, (t + 1) * VS)
                one, two = (acc[:, (2 * par + i) * H:(2 * par + i + 1) * H] for i in range(2))
                dve.tensor_tensor(one, one, two, ALU.add).then_inc(sum_half, 1)
                dve.wait_ge(sum_half, t + 1)
                dve.wait_ge(p_add, (t + 1) * GA)
                wait(dve, g_done, t - 1)
                dve.tensor_tensor(x2t[:, par * H:(par + 1) * H], one, pacc[:, par * H:(par + 1) * H],
                                  ALU.add).then_inc(x2_ready, 1)

            def chunk(c, prep, layer1):
                for u in range(KT * NQ):
                    k, q = divmod(u, NQ)
                    if prep and u == prep_at(c, 1):
                        split(c + NG)
                    if layer1 and u == U_X0TED:
                        x0t_evac(c + 1)
                    if layer1 and u in U_PROD:
                        product(c + 1, U_PROD.index(u))
                    if q == Q_SUM and not (k == 0 and isinstance(c, int) and c == 0):
                        sum_tile(c * KT + k - 1, (k - 1) % KT)
                    if WHO[q] == "V":
                        weigh(c, k, q)
                    if layer1 and u == U_X1L:
                        x1_lo_out(c + 1, 0, KT - 1, 1)
                    if layer1 and u == U_Z1:
                        z1_out(c + 1)
                if layer1:
                    x1_lo_out(c + 1, KT - 1, KT, 2)

            for n in range(NG):
                split(n)
            for j in range(NJ):
                product(0, j)
                if j == 0:
                    x0t_evac(0)
            x1_lo_out(0, 0, KT - 1, 1)
            z1_out(0)
            x1_lo_out(0, KT - 1, KT, 2)
            chunk(0, True, True)
            with dve.Fori(1, NC - NG) as c:
                chunk(c, True, True)
            with dve.Fori(NC - NG, NC - 1) as c:
                chunk(c, False, True)
            chunk(NC - 1, False, False)
            sum_tile(NT - 1, KT - 1)
            dve.wait_ge(dense_out, 2)
            for j in range(1, J1, 2):
                dve.wait_ge(h1_done, j + 1)
                dve.tensor_scalar(h1[:, j * B:(j + 1) * B], h1_bank[j][:, :], b1c[:, j:j + 1], 0.0,
                                  ALU.add, ALU.max).then_inc(h1_dve, 1)
            dve.wait_ge(h2_done, 2)
            dve.tensor_scalar(h2[:, B:2 * B], h2_bank[1][:, :], b2c[:, 1:2], 0.0,
                              ALU.add, ALU.max).then_inc(h2_dve, 1)
            dve.wait_ge(y_done, 1)
            dve.tensor_copy(y_row, g_bank[0:1, 0:B]).then_inc(y_copied, 1)

        @block.tensor
        def _(pe):
            def setup_turn(i):
                kind, g = GROUPS[i]
                if i >= NY:
                    j = i - NY
                    if GROUPS[j][0] == "k1":
                        pe.wait_ge(dve_setup, G_K1.index(j) + 1)
                    else:
                        pe.wait_ge(act_setup, j + 1)
                if kind == "k0":
                    pe.wait_ge(w0_ready, 2 * NS - 1)
                    pe.wait_ge(consts, 1)
                    for b in range(min(4, NJ - 4 * g)):
                        j = 4 * g + b
                        last = pe.transpose(y_bank[i % NY][0:PB, b * H:(b + 1) * H],
                                            w0_pre[:, j * PB:(j + 1) * PB], ident[:, :])
                else:
                    raw, arrived = (k1_raw, k1_in) if kind == "k1" else (k2_raw, k2_in)
                    pe.wait_ge(arrived, 16)
                    for b in range(UM):
                        m = g * UM + b
                        last = pe.transpose(y_bank[i % NY][:, b * H:(b + 1) * H],
                                            raw[:, m:m + (H - 1) * M + 1:M], ident[:, :])
                last.then_inc(turned_k, 1)

            def turn(n, c):
                pe.wait_ge(split_lo, n + 1)
                wait(pe, turn_out, n)
                wait(pe, prod_done, c * NJ - 1)
                for d in range(DG):
                    last = pe.transpose(ring[0][0:2 * M, d * P:(d + 1) * P],
                                        halves[:, d * 2 * M:(d + 1) * 2 * M], ident[:, :])
                last.then_inc(turned, 1)

            def columns(c):
                return xs[:, bass.ds((c % 8) * CW, CW)]

            def base_select(c, prep):
                pe.wait_ge(turn_out, (c // KT + 1) * NG)
                if isinstance(c, int) and c == 0:
                    pe.wait_ge(sel_ready, 1)
                wait(pe, prod_done, c * NJ)
                pe.matmul(ring[1][0:PB, :], sel[:, 0:PB], columns(c), start=True, stop=True).then_inc(based, 1)

            def shift_select(c, j, prep):
                if j == 0:
                    if prep:
                        pe.wait_ge(turn_out, NG if isinstance(c, int) and c < 2 else c + NG)
                    wait(pe, prod_done, c * NJ - 1)
                elif j == 2:
                    pe.wait_ge(x0t_out, c + 1)
                elif j == 1:
                    pe.wait_ge(prod_done, c * NJ + 1)
                else:
                    pe.wait_ge(prod_done, c * NJ + j - 1)
                pe.matmul(ring[SHIFT_BANK[j]][0:PB, :], sel[:, (1 + j) * PB:(2 + j) * PB], columns(c),
                          start=True, stop=True).then_inc(shifted, 1)

            def x0_turn(c):
                pe.wait_ge(base_out, c + 1)
                for k in range(KT):
                    last = pe.transpose(ring[1][:, k * PB:(k + 1) * PB], base[:, k * P:(k + 1) * P],
                                        ident[0:PB, 0:PB])
                last.then_inc(x0_turned, 1)

            def fold(c, j):
                pe.wait_ge(prod_done, c * NJ + j + 1)
                if j == 0:
                    wait(pe, x1l_done, 2 * c)
                b = prod_slot(j)
                pe.matmul(x_bank[:, :], w0_t[:, j * H:(j + 1) * H], prod[0:PB, b * CW:(b + 1) * CW],
                          start=(j == 0), stop=(j == NJ - 1)).then_inc(folded, 1)

            def unit(c, k, q):
                t = c * KT + k
                u = k * NQ + q
                if q == 0:
                    pe.wait_ge(x1l_done, 2 * c + (2 if k == KT - 1 else 1))
                if u >= NY:
                    s, n = freed_by((u - NY) % NQ, c * KT + (u - NY) // NQ)
                else:
                    s, n = freed_by((u - NY) % NQ, (c - 1) * KT + (KT * NQ + u - NY) // NQ)
                wait(pe, s, n)
                bank = y_bank[u % NY][:, :]
                hi, lo = x1_hi[:, k * P:(k + 1) * P], x1_lo[:, k * P:(k + 1) * P]
                s = slice(q * CW, (q + 1) * CW)
                pe.matmul(bank, hi, k1_lo[:, s], start=True, stop=False)
                pe.matmul(bank, hi, k1_hi[:, s], start=False, stop=False)
                pe.matmul(bank, lo, k1_hi[:, s], start=False, stop=True).then_inc(y_ready, 1)

            def g_matmul(t, k):
                par = k % 2
                pe.wait_ge(x2_ready, t + 1)
                pe.wait_ge(diag_ready, t + 1)
                wait(pe, g_out, t)
                pe.matmul(g_bank[:, 0:TB * M1], x2t[:, par * H:(par + 1) * H], diag[:, :],
                          start=True, stop=True).then_inc(g_done, 1)

            def chunk(c, prep, layer1):
                for u in range(KT * NQ):
                    k, q = divmod(u, NQ)
                    if prep and u == prep_at(c, 2):
                        turn(c + NG, c + 2 if isinstance(c, int) and c == 0 else c + 1)
                    if layer1:
                        if u == U_BASE:
                            base_select(c + 1, prep)
                        if u == U_X0T:
                            x0_turn(c + 1)
                        if u in U_SHIFT:
                            shift_select(c + 1, U_SHIFT.index(u), prep)
                        if u in U_FOLD:
                            fold(c + 1, U_FOLD.index(u))
                    if q == Q_G and not (k == 0 and isinstance(c, int) and c == 0):
                        g_matmul(c * KT + k - 1, (k - 1) % KT)
                    unit(c, k, q)

            for i in range(len(GROUPS)):
                setup_turn(i)
            for n in range(NG):
                turn(n, 0)
            base_select(0, True)
            shift_select(0, 0, True)
            x0_turn(0)
            for j in range(1, NJ):
                shift_select(0, j, True)
                if j >= 2:
                    fold(0, j - 2)
            fold(0, NJ - 2)
            fold(0, NJ - 1)
            pe.wait_ge(act_setup, len(GROUPS))
            pe.wait_ge(dve_setup, NQ)
            chunk(0, True, True)
            with pe.Fori(1, NC - NG) as c:
                chunk(c, True, True)
            with pe.Fori(NC - NG, NC - 1) as c:
                chunk(c, False, True)
            chunk(NC - 1, False, False)
            g_matmul(NT - 1, KT - 1)
            pe.wait_ge(small_in, 64)
            pe.transpose(ring[1][:, 0:J1 + 2 * J2], rows[:, :], ident[0:J1 + 2 * J2, 0:J1 + 2 * J2])
            for t in range(NBT):
                last = pe.transpose(ring[0][0:ND, t * P:(t + 1) * P], dense[:, t * ND:(t + 1) * ND], ident[:, :])
            last.then_inc(dense_done, 1)
            pe.wait_ge(g_out, NT)
            pe.wait_ge(a_unit, NT * NA)
            pe.wait_ge(v_step, NT * VS)
            for m in range(M):
                last = pe.matmul(y_bank[0][:, :], k2_t[:, m * H:(m + 1) * H], G[:, m, :],
                                 start=(m == 0), stop=(m == M - 1))
            last.then_inc(z3_done, 1)
            pe.wait_ge(w_in, 32)
            pe.wait_ge(dense_out, 2)
            pe.wait_ge(z1_done, NC)
            for j in range(J1):
                s = slice(j * P, (j + 1) * P)
                pe.matmul(h1_bank[j][:, :], w1[:, s], z1[:, :], start=True, stop=False)
                pe.matmul(h1_bank[j][:, :], w1[:, N1 + j * P:N1 + (j + 1) * P], G[:, M, :], start=False, stop=False)
                pe.matmul(h1_bank[j][:, :], w1d[:, s], dense_t, start=False, stop=False)
            pe.wait_ge(z3_out, 1)
            for j in range(J1):
                pe.matmul(h1_bank[j][:, :], w1[:, 2 * N1 + j * P:2 * N1 + (j + 1) * P], z3,
                          start=False, stop=True).then_inc(h1_done, 1)
            pe.wait_ge(w2_in, 16)
            for i in range(J2):
                for j in range(J1):
                    if i == 0:
                        pe.wait_ge(*((h1_act, j // 2 + 1) if j % 2 == 0 else (h1_dve, j // 2 + 1)))
                    last = pe.matmul(h2_bank[i][:, :], w2[:, j * N2 + i * P:j * N2 + (i + 1) * P],
                                     h1[:, j * B:(j + 1) * B], start=(j == 0), stop=(j == J1 - 1))
                last.then_inc(h2_done, 1)
            pe.wait_ge(h2_act, 1)
            pe.matmul(g_bank[0:1, 0:B], w3c[:, 0:1], h2[:, 0:B], start=True, stop=False)
            pe.wait_ge(h2_dve, 1)
            pe.matmul(g_bank[0:1, 0:B], w3c[:, 1:2], h2[:, B:2 * B], start=False, stop=True).then_inc(y_done, 1)


N_TABLES = 40
_INS = ["dense_ctx", "ids"] + [f"tbl_{i}" for i in range(N_TABLES)] + \
       ["W_top1", "b_top1", "W_top2", "b_top2", "W_top3", "L0_rec_k0", "L0_rec_k1", "L0_rec_k2"]


def kernel(**inputs):
    import numpy as _np
    import concourse.bacc as _bacc
    from concourse import mybir as _mybir
    from concourse.bass_utils import run_bass_kernel_spmd as _run

    nc = _bacc.Bacc("TRN2", target_bir_lowering=False, num_devices=1)
    arrays, aps = {}, {}
    for name in _INS:
        a = _np.ascontiguousarray(inputs[name])
        arrays[f"in_{name}_dram"] = a
        aps[name] = nc.dram_tensor(f"in_{name}_dram", a.shape, _mybir.dt.from_np(a.dtype), kind="ExternalInput").ap()
    out = nc.dram_tensor("out_0_dram", (aps["ids"].shape[0], 1), _mybir.dt.float32, kind="ExternalOutput").ap()
    cin_tower(nc, aps["dense_ctx"], aps["ids"], [aps[f"tbl_{i}"] for i in range(N_TABLES)],
              aps["W_top1"], aps["b_top1"], aps["W_top2"], aps["b_top2"], aps["W_top3"],
              aps["L0_rec_k0"], aps["L0_rec_k1"], aps["L0_rec_k2"], out)
    r = _run(nc, [arrays], core_ids=[0])
    return r.results[0]["out_0_dram"]
```

```python
import concourse.bass as bass
from concourse import mybir
from contextlib import ExitStack



def cin_tower(nc, dense_ctx, ids, tables, W_top1, b_top1, W_top2, b_top2, W_top3, k0, k1, k2, out):
    fp32 = mybir.dt.float32
    fp32r = mybir.dt.float32r
    i32 = mybir.dt.int32
    u32 = mybir.dt.uint32
    ALU = mybir.AluOpType
    ACT = mybir.ActivationFunctionType
    AX = mybir.AxisListType

    B, M = ids.shape
    D = tables[0].shape[1]
    H = k1.shape[0]
    P = 128
    NBT = B // P
    CB = 32
    CW = CB * D
    NC = B // CB
    TB = P // D
    KT = CW // P
    NT = NC * KT
    SH = 3
    PB = SH * M
    NJ = (M // 2 + 1) // SH
    NS = NJ * SH
    UM = CW // H
    NQ = M // UM
    M1 = M + 1
    DG = 4
    NG = D // DG
    N1, N2 = W_top1.shape[1], W_top2.shape[1]
    J1, J2 = N1 // P, N2 // P
    ND = dense_ctx.shape[1]

    WHO = "VAVAVVAVAV"
    V_UNITS = [q for q in range(NQ) if WHO[q] == "V"]
    A_UNITS = [q for q in range(NQ) if WHO[q] == "A"]
    NV, NA = len(V_UNITS), len(A_UNITS)
    VS = NV * UM
    GA = NA + 1
    NY = 4
    NP = 2
    NR = 2
    EARLY = 24
    GATHER_TILES = [5, 11, 16]

    U_TURN, U_TURNED = 5, 6
    U_TURN_1, U_TURNED_1 = [24, 32], [26, 34]
    U_X0T = 29
    U_PROD = [9, 12, 15, 18, 21, 24, 27]
    U_FOLD = [u + 4 for u in U_PROD]
    U_Z1 = 2
    U_X1H, U_X1L = 34, 36
    Q_SUM, Q_G, Q_GOUT = 4, 8, 9
    Q_X0C = 7

    ctx = ExitStack()
    with ctx:
        def sb(name, shape, dt=fp32):
            return ctx.enter_context(nc.sbuf_tensor(name, shape, dt))

        def sem(name):
            return ctx.enter_context(nc.semaphore(name))

        region = sb("region", [P, M1 * B])
        G = region[:, :].rearrange("p (m b) -> p m b", m=M1)
        at = [0]

        def carve(n):
            at[0] += n
            assert at[0] <= M1 * B
            return region[:, at[0] - n:at[0]]
        k0_raw = carve(M * M)
        k1_raw = carve(H * M)
        k2_raw = carve(H * M)
        w0_pre = carve(NS * M)


        k1_hi = sb("k1_hi", [P, M * H], fp32r)
        k1_lo = sb("k1_lo", [P, M * H], fp32r)
        k2_t = sb("k2_t", [P, M * H])
        w0_t = sb("w0_t", [PB, NJ * H])
        ident = sb("ident", [P, P])
        row_mask = sb("row_mask", [P, TB])
        idx = sb("idx", [P, NBT * M], i32)
        emb = sb("emb", [P, M * NBT * D])
        stage = sb("stage", [P, DG * PB])
        et = sb("et", [PB, 2 * P * D])
        shift = sb("shift", [PB, NR * CW])
        base = sb("base", [PB, CW])
        prod = sb("prod", [P, NP * CW])
        x0c = sb("x0c", [P, 2 * M1])
        x1_hi = sb("x1_hi", [P, CW], fp32r)
        x1_lo = sb("x1_lo", [P, CW], fp32r)
        acc = sb("acc", [P, 2 * 2 * H])
        x2t = sb("x2t", [P, 2 * H])
        zw = sb("zw", [P, NA * CW])
        psum4 = sb("psum4", [P, CW])
        pacc = sb("pacc", [P, 2 * H])
        diag = sb("diag", [P, TB * M1])
        z1 = sb("z1", [P, B])
        cols = sb("cols", [P, J1 + 2 * J2])
        b1c, b2c, w3c = cols[:, 0:J1], cols[:, J1:J1 + J2], cols[:, J1 + J2:]
        dense_t = base[0:ND, 0:B]
        w1 = zw[:, 0:3 * N1]
        w1d = psum4[0:ND, 0:N1]
        h1 = emb[:, 0:J1 * B]
        dense = emb[:, J1 * B:J1 * B + NBT * ND]
        rows = emb[0:J1 + 2 * J2, J1 * B + NBT * ND:J1 * B + NBT * ND + P]
        stage0 = zw[:, 0:D * PB].rearrange("p (d f) -> p d f", d=D)
        z3 = prod[:, 0:B]
        h2 = k2_t[:, 0:J2 * B]
        w2 = k2_t[:, J2 * B:J2 * B + J1 * N2]
        y_row = acc[0:1, 0:B]

        y_bank = [ctx.enter_context(nc.psum_tensor(f"y_bank{i}", [P, CW], fp32)) for i in range(NY)]
        ring = [ctx.enter_context(nc.psum_tensor(f"ring{i}", [P, CW], fp32)) for i in range(2)]
        x_bank = ctx.enter_context(nc.psum_tensor("x_bank", [P, CW], fp32))
        g_bank = ctx.enter_context(nc.psum_tensor("g_bank", [P, CW], fp32))

        ids_in = sem("ids_in")
        k0_in, k1_in, k2_in = sem("k0_in"), sem("k1_in"), sem("k2_in")
        small_in = sem("small_in")
        w_in, w2_in = sem("w_in"), sem("w2_in")
        gathered = sem("gathered")
        consts = sem("consts")
        const_step = sem("const_step")
        w0_step, w0_ready = sem("w0_step"), sem("w0_ready")
        turned_k = sem("turned_k")
        act_setup, dve_setup = sem("act_setup"), sem("dve_setup")
        ones_ready = sem("ones_ready")
        staged0_dve, staged0_act, staged = sem("staged0_dve"), sem("staged0_act"), sem("staged")
        turned, turn_out = sem("turned"), sem("turn_out")
        base_in = sem("base_in")
        shift_in = [sem(f"shift_in{i}") for i in range(NR)]
        prod_done = sem("prod_done")
        x0_turned = sem("x0_turned")
        folded = sem("folded")
        x1h_done, x1l_done, z1_done = sem("x1h_done"), sem("x1l_done"), sem("z1_done")
        y_ready = sem("y_ready")
        v_step, a_unit, p_add = sem("v_step"), sem("a_unit"), sem("p_add")
        x0c_ready, diag_ready = sem("x0c_ready"), sem("diag_ready")
        sum_half, x2_ready = sem("sum_half"), sem("x2_ready")
        g_done, g_out = sem("g_done"), sem("g_out")
        z3_done, z3_out = sem("z3_done"), sem("z3_out")
        dense_done, dense_out = sem("dense_done"), sem("dense_out")
        h1_done, h1_act, h1_dve = sem("h1_done"), sem("h1_act"), sem("h1_dve")
        h2_done, h2_act, h2_dve = sem("h2_done"), sem("h2_act"), sem("h2_dve")
        y_done, y_copied, y_stored = sem("y_done"), sem("y_copied"), sem("y_stored")

        def wait(eng, s, n):
            if isinstance(n, int) and n <= 0:
                return
            eng.wait_ge(s, n)

        def freed_by(q, t):
            if q in V_UNITS:
                return v_step, t * VS + UM * (V_UNITS.index(q) + 1)
            return a_unit, t * NA + A_UNITS.index(q) + 1

        W0_OPS = sum(len({0, s % SH, (s % SH - s) % M, M}) - 1 for s in range(NS))
        GROUPS = [("k0", g) for g in range(-(-NJ // 4))] + [("k1", g) for g in range(NQ)] + \
                 [("k2", g) for g in range(NQ)]
        G_K1 = [i for i, g in enumerate(GROUPS) if g[0] == "k1"]
        G_ACT = [i for i, g in enumerate(GROUPS) if g[0] != "k1" or True]

        def emb_step(n):
            return emb[:, :].rearrange("p (f r) -> p f r", f=M)[:, :, bass.ds(n * DG, DG)].rearrange("p f d -> p d f")

        def prod_slot(j):
            return j % NP

        PER_SLOT = (NJ - 1) // NR
        assert PER_SLOT * NR == NJ - 1

        def shift_slot(j):
            return (j - 1) % NR

        def shift_value(c, j):
            return (c * PER_SLOT + (j - 1) // NR + 1) * (16 * 2)

        def e_columns(c):
            return et[:, bass.ds((c % (2 * KT)) * CW, CW)]

        h1_bank = [y_bank[1], y_bank[2], y_bank[3], x_bank]
        h2_bank = [ring[0], ring[1]]
        emb_tile0 = emb[:, :].rearrange("p (f r) -> p f r", f=M)[:, :, 0:D].rearrange("p f d -> p d f")
        stage_v = stage[:, :].rearrange("p (d f) -> p d f", d=DG)

        def thrice(v):
            return v.rearrange("p d (n f) -> p n d f", n=SH)

        def first_stage(g):
            d = slice(g * DG, (g + 1) * DG)
            return thrice(stage0[:, d, :]), emb_tile0[:, d, :].unsqueeze(1).broadcast_to([P, SH, DG, M])

        def turn_bank(n):
            return ring[n % 2] if isinstance(n, int) and n < NG else ring[0]

        def preps(c):
            if not isinstance(c, int):
                return [(c + NG, U_TURN, U_TURNED)]
            if c == 1:
                return [(NG + i, U_TURN_1[i], U_TURNED_1[i]) for i in range(2)]
            return []

        block = ctx.enter_context(nc.Block())

        @block.sync
        def _(sp):
            sp.dma_start(idx[:, :].rearrange("p (t f) -> p t f", t=NBT),
                         ids.rearrange("(t p) f -> p t f", p=P)).then_inc(ids_in, 16)
            sp.dma_start(k0_raw, k0.rearrange("o h m -> o (h m)")).then_inc(k0_in, 16)
            sp.dma_start(k1_raw, k1.rearrange("o h m -> o (h m)")).then_inc(k1_in, 16)
            sp.dma_start(k2_raw, k2.rearrange("o h m -> o (h m)")).then_inc(k2_in, 16)
            def copy_rows(dst, first, n, row, column, done):
                sp.dma_start(dst[first:first + n, :], et[row:row + n, bass.ds(column, CW)]).then_inc(done, 16)

            def spread(c):
                column = (c % (2 * KT)) * CW
                if not isinstance(c, int):
                    column = sp.snap(column)
                wait(sp, prod_done, c * NJ)
                sp.wait_ge(turn_out, (c // KT + 1) * NG)
                wait(sp, x0_turned, c)
                for n in range(SH):
                    copy_rows(base[:, :], n * M, M, (M - n) % M, column, base_in)
                for j in range(1, NJ):
                    if j > NR:
                        sp.wait_ge(prod_done, c * NJ + j - NR + 1)
                    b = shift_slot(j)
                    to = shift[:, b * CW:(b + 1) * CW]
                    copy_rows(to, 0, PB - SH * j, SH * j, column, shift_in[b])
                    copy_rows(to, PB - SH * j, SH * j, 0, column, shift_in[b])

            spread(0)
            spread(1)
            with sp.Fori(2, NC) as c:
                spread(c)
            sp.wait_ge(p_add, NT * GA)
            sp.dma_start(w1.rearrange("p (j n) -> p j n", j=3),
                         W_top1[0:3 * H, :].rearrange("(j p) n -> p j n", p=P)).then_inc(w_in, 16)
            sp.dma_start(w1d, W_top1[3 * H:3 * H + ND, :]).then_inc(w_in, 16)
            sp.dma_start(rows[0:J1, :], b_top1.rearrange("(j p) -> j p", p=P)).then_inc(small_in, 16)
            sp.dma_start(rows[J1:J1 + J2, :], b_top2.rearrange("(j p) -> j p", p=P)).then_inc(small_in, 16)
            sp.dma_start(rows[J1 + J2:J1 + 2 * J2, :],
                         W_top3.rearrange("(j p) n -> j (p n)", p=P)).then_inc(small_in, 16)
            sp.dma_start(dense.rearrange("p (t n) -> p t n", t=NBT),
                         dense_ctx.rearrange("(t p) n -> p t n", p=P)).then_inc(small_in, 16)
            sp.wait_ge(z3_done, 1)
            sp.dma_start(w2.rearrange("p (j n) -> p j n", j=J1),
                         W_top2.rearrange("(j p) n -> p j n", p=P)).then_inc(w2_in, 16)
            sp.wait_ge(y_copied, 1)
            sp.dma_start(out.rearrange("b n -> n b"), y_row).then_inc(y_stored, 16)
            sp.wait_ge(y_stored, 16)

        @block.gpsimd
        def _(pool):
            pool.memset(ident[:, :], 0.0).then_inc(const_step, 1)
            pool.wait_ge(const_step, 1)
            pool.affine_select(out=ident[:, :], in_=ident[:, :], compare_op=ALU.not_equal, fill=1.0,
                               base=0, pattern=[[-1, P]], channel_multiplier=1).then_inc(consts, 1)

            def gather(t, features):
                if 0 in features:
                    wait(pool, gathered, 16 * M * t)
                for f in features:
                    a = (f * NBT + t) * D
                    pool.indirect_dma_start(
                        out=emb[:, a:a + D], out_offset=None, in_=tables[f],
                        in_offset=bass.IndirectOffsetOnAxis(
                            ap=idx[:, t * M + f:t * M + f + 1].bitcast(u32), axis=0),
                    ).then_inc(gathered, 16)

            pool.wait_ge(ids_in, 16)
            gather(0, range(M))

            pool.memset(row_mask[:, :], 1.0).then_inc(const_step, 1)
            steps = 2
            pool.wait_ge(const_step, steps)
            pool.affine_select(out=row_mask[:, :], in_=row_mask[:, :], compare_op=ALU.is_ge, fill=0.0,
                               base=0, pattern=[[-D, TB]], channel_multiplier=1).then_inc(const_step, 1)
            steps += 1
            pool.wait_ge(const_step, steps)
            pool.affine_select(out=row_mask[:, :], in_=row_mask[:, :], compare_op=ALU.is_ge, fill=0.0,
                               base=D - 1, pattern=[[D, TB]], channel_multiplier=-1).then_inc(const_step, 1)
            steps += 1
            gather(1, range(EARLY))

            def diagonal(c, k):
                t = c * KT + k
                pool.wait_ge(x0c_ready, t + 1)
                wait(pool, g_done, t)
                if isinstance(c, int) and t == 0:
                    pool.wait_ge(const_step, steps)
                par = k % 2
                shape = [P, TB, M1]
                pool.tensor_tensor(
                    diag[:, :].rearrange("p (b m) -> p b m", b=TB),
                    x0c[:, par * M1:(par + 1) * M1].unsqueeze(1).broadcast_to(shape),
                    row_mask[:, :].unsqueeze(2).broadcast_to(shape), ALU.mult).then_inc(diag_ready, 1)

            def add_units(c, k):
                t = c * KT + k
                for a in range(1, NA):
                    pool.wait_ge(a_unit, t * NA + a + 1)
                    if a == 1:
                        one = zw[:, 0:CW]
                        wait(pool, p_add, t * GA)
                    else:
                        one = psum4[:, :]
                        pool.wait_ge(p_add, t * GA + a - 1)
                    pool.tensor_tensor(psum4[:, :], one, zw[:, a * CW:(a + 1) * CW], ALU.add).then_inc(p_add, 1)
                pool.wait_ge(p_add, t * GA + NA - 1)
                pool.tensor_tensor(psum4[:, 0:CW // 2], psum4[:, 0:CW // 2], psum4[:, CW // 2:CW], ALU.add).then_inc(p_add, 1)
                pool.wait_ge(p_add, t * GA + NA)
                wait(pool, x2_ready, t - 1)
                par = k % 2
                pool.tensor_tensor(pacc[:, par * H:(par + 1) * H], psum4[:, 0:H], psum4[:, H:2 * H],
                                   ALU.add).then_inc(p_add, 1)

            def chunk(c, gathers=()):
                for k in range(KT):
                    for part in gathers[k:k + 1]:
                        gather(*part)
                    add_units(c, k)
                    diagonal(c, k)

            part_of = []
            for t, tiles in zip(range(1, NBT), GATHER_TILES):
                first = EARLY if t == 1 else 0
                cut_at = [first + (M - first) * i // tiles for i in range(tiles + 1)]
                part_of += [(t, range(cut_at[i], cut_at[i + 1])) for i in range(tiles)]
            assert len(part_of) % KT == 0
            for c in range(len(part_of) // KT):
                chunk(c, part_of[c * KT:(c + 1) * KT])
            with pool.Fori(len(part_of) // KT, NC) as c:
                chunk(c)

        @block.scalar
        def _(act):
            def setup_out(i):
                kind, g = GROUPS[i]
                act.wait_ge(turned_k, i + 1)
                src = y_bank[i % NY]
                if kind == "k0":
                    n = min(4, NJ - 4 * g) * H
                    act.activation(w0_t[:, 4 * g * H:4 * g * H + n], src[0:PB, 0:n], ACT.Copy).then_inc(act_setup, 1)
                elif kind == "k1":
                    act.activation(k1_hi[:, g * CW:(g + 1) * CW], src[:, :], ACT.Copy).then_inc(act_setup, 1)
                else:
                    act.activation(k2_t[:, g * CW:(g + 1) * CW], src[:, :], ACT.Copy).then_inc(act_setup, 1)

            def stage_e(n):
                act.wait_ge(gathered, (n // NG + 1) * (16 * M))
                wait(act, turned, n)
                e = emb_step(n)
                act.activation(thrice(stage_v), e.unsqueeze(1).broadcast_to([P, SH, DG, M]), ACT.Copy).then_inc(staged, 1)

            def turn_evac(n, c):
                act.wait_ge(turned, n + 1)
                wait(act, prod_done, c * NJ)
                v = et[:, :].rearrange("p (r b g e) -> p r g b e", r=2, b=P, g=NG)
                act.activation(v[:, (n // NG) % 2, n % NG, :, :],
                               turn_bank(n)[0:PB, :].rearrange("p (e b) -> p b e", e=DG),
                               ACT.Copy).then_inc(turn_out, 1)

            def x0c_copy(c, k):
                t = c * KT + k
                act.wait_ge(x0_turned, c + 1)
                if isinstance(c, int) and c + k == 0:
                    act.wait_ge(ones_ready, 1)
                wait(act, v_step, (t - 1) * VS)
                wait(act, diag_ready, t - 1)
                par = k % 2
                act.activation(x0c[:, par * M1:par * M1 + M], ring[1][:, k * PB:k * PB + M], ACT.Copy).then_inc(x0c_ready, 1)

            def x1_hi_out(c, k0_, k1_):
                act.wait_ge(folded, NJ * (c + 1))
                wait(act, y_ready, ((c - 1) * KT + k1_) * NQ)
                if k0_:
                    act.wait_ge(x1l_done, 2 * c + 1)
                s = slice(k0_ * P, k1_ * P)
                act.activation(x1_hi[:, s], x_bank[:, s], ACT.Copy).then_inc(x1h_done, 1)

            def weigh(c, k, q):
                t = c * KT + k
                a = A_UNITS.index(q)
                act.wait_ge(y_ready, t * NQ + q + 1)
                if a == 0:
                    act.wait_ge(x0c_ready, t + 1)
                wait(act, p_add, (t - 1) * GA + max(a, 1))
                par = k % 2
                for i in range(UM):
                    m = q * UM + i
                    last = act.activation(zw[:, a * CW + i * H:a * CW + (i + 1) * H],
                                          y_bank[(k * NQ + q) % NY][:, i * H:(i + 1) * H], ACT.Copy,
                                          scale=x0c[:, par * M1 + m:par * M1 + m + 1])
                last.then_inc(a_unit, 1)

            def g_evac(t):
                act.wait_ge(g_done, t + 1)
                act.activation(G[:, :, bass.ds(t * TB, TB)],
                               g_bank[:, 0:TB * M1].rearrange("p (b m) -> p m b", b=TB),
                               ACT.Copy).then_inc(g_out, 1)

            def chunk(c, prep, layer1):
                for u in range(KT * NQ):
                    k, q = divmod(u, NQ)
                    for n, u_turn, u_out in preps(c) if prep else ():
                        if u == u_turn - 3:
                            stage_e(n)
                        if u == u_out:
                            turn_evac(n, c)
                    if q == Q_X0C:
                        if k < KT - 1:
                            x0c_copy(c, k + 1)
                        elif layer1:
                            x0c_copy(c + 1, 0)
                    if q == Q_GOUT and not (k == 0 and isinstance(c, int) and c == 0):
                        g_evac(c * KT + k - 1)
                    if WHO[q] == "A":
                        weigh(c, k, q)
                    if layer1 and u == U_X1H:
                        x1_hi_out(c + 1, 0, KT - 1)
                if layer1:
                    x1_hi_out(c + 1, KT - 1, KT)

            for i in range(len(GROUPS)):
                setup_out(i)
            act.wait_ge(gathered, 16 * M)
            for g in range(1, NG, 2):
                act.activation(*first_stage(g), ACT.Copy).then_inc(staged0_act, 1)
            for n in range(NG):
                turn_evac(n, 0)
            x0c_copy(0, 0)
            x1_hi_out(0, 0, KT - 1)
            x1_hi_out(0, KT - 1, KT)
            chunk(0, True, True)
            chunk(1, True, True)
            with act.Fori(2, NC - NG) as c:
                chunk(c, True, True)
            with act.Fori(NC - NG, NC - 1) as c:
                chunk(c, False, True)
            chunk(NC - 1, False, False)
            g_evac(NT - 1)
            act.wait_ge(small_in, 64)
            act.wait_ge(dense_done, 1)
            act.activation(dense_t, ring[0][0:ND, 0:B], ACT.Copy).then_inc(dense_out, 1)
            act.activation(cols[:, :], ring[1][:, 0:J1 + 2 * J2], ACT.Copy).then_inc(dense_out, 1)
            act.wait_ge(dense_out, 2)
            act.wait_ge(z3_done, 1)
            act.activation(z3, y_bank[0][:, :], ACT.Copy).then_inc(z3_out, 1)
            for j in range(0, J1, 2):
                act.wait_ge(h1_done, j + 1)
                act.activation(h1[:, j * B:(j + 1) * B], h1_bank[j][:, :], ACT.Relu,
                               bias=b1c[:, j:j + 1]).then_inc(h1_act, 1)
            act.wait_ge(h2_done, 1)
            act.activation(h2[:, 0:B], h2_bank[0][:, :], ACT.Relu, bias=b2c[:, 0:1]).then_inc(h2_act, 1)

        @block.vector
        def _(dve):
            dve.memset(x0c[:, :], 1.0).then_inc(ones_ready, 1)
            dve.wait_ge(k0_in, 16)
            for s in range(NS):
                n = s % SH
                ends = sorted({0, n, (n - s) % M, M})
                for lo, hi in zip(ends, ends[1:]):
                    i, j = (lo - n) % M, (lo - n + s) % M
                    dst = w0_pre[:, s * M + lo:s * M + hi]
                    one, two = (k0_raw[:, a:a + (hi - lo - 1) * (M + 1) + 1:M + 1] for a in (i * M + j, j * M + i))
                    if s == 0 or 2 * s == M:
                        dve.tensor_copy(dst, one).then_inc(w0_ready, 1)
                    else:
                        dve.tensor_tensor(dst, one, two, ALU.add).then_inc(w0_ready, 1)
            for i in G_K1:
                g = GROUPS[i][1]
                dve.wait_ge(act_setup, i + 1)
                s = slice(g * CW, (g + 1) * CW)
                dve.tensor_tensor(k1_lo[:, s], y_bank[i % NY][:, :], k1_hi[:, s].bitcast(fp32),
                                  ALU.subtract).then_inc(dve_setup, 1)

            def product(c, j):
                if j == 0:
                    dve.wait_ge(base_in, (c + 1) * (16 * SH))
                    other = e_columns(c)
                else:
                    dve.wait_ge(shift_in[shift_slot(j)], shift_value(c, j))
                    a = shift_slot(j)
                    other = shift[:, a * CW:(a + 1) * CW]
                wait(dve, folded, c * NJ + j - NP + 1)
                b = prod_slot(j)
                dve.tensor_tensor(prod[0:PB, b * CW:(b + 1) * CW], base[:, :], other,
                                  ALU.mult).then_inc(prod_done, 1)

            def x1_lo_out(c, k0_, k1_, n):
                dve.wait_ge(x1h_done, 2 * c + n)
                s = slice(k0_ * P, k1_ * P)
                dve.tensor_tensor(x1_lo[:, s], x_bank[:, s], x1_hi[:, s].bitcast(fp32),
                                  ALU.subtract).then_inc(x1l_done, 1)

            def z1_out(c):
                dve.tensor_reduce(z1[:, bass.ds(c * CB, CB)], x_bank[:, :].rearrange("p (b d) -> p b d", b=CB),
                                  AX.X, ALU.add).then_inc(z1_done, 1)

            def weigh(c, k, q):
                t = c * KT + k
                v = V_UNITS.index(q)
                par = k % 2
                dve.wait_ge(y_ready, t * NQ + q + 1)
                if v == 0:
                    dve.wait_ge(x0c_ready, t + 1)
                    wait(dve, x2_ready, t - 1)
                for i in range(UM):
                    n = v * UM + i
                    m = q * UM + i
                    a = acc[:, (2 * par + n % 2) * H:(2 * par + n % 2 + 1) * H]
                    y = y_bank[(k * NQ + q) % NY][:, i * H:(i + 1) * H]
                    e = x0c[:, par * M1 + m:par * M1 + m + 1]
                    if n < 2:
                        dve.tensor_scalar(a, y, e, None, ALU.mult).then_inc(v_step, 1)
                    else:
                        dve.wait_ge(v_step, t * VS + n - 1)
                        dve.scalar_tensor_tensor(out=a, in0=y, scalar=e, in1=a, op0=ALU.mult,
                                                 op1=ALU.add).then_inc(v_step, 1)

            def sum_tile(t, k):
                par = k % 2
                dve.wait_ge(v_step, (t + 1) * VS)
                one, two = (acc[:, (2 * par + i) * H:(2 * par + i + 1) * H] for i in range(2))
                dve.tensor_tensor(one, one, two, ALU.add).then_inc(sum_half, 1)
                dve.wait_ge(sum_half, t + 1)
                dve.wait_ge(p_add, (t + 1) * GA)
                wait(dve, g_done, t - 1)
                dve.tensor_tensor(x2t[:, par * H:(par + 1) * H], one, pacc[:, par * H:(par + 1) * H],
                                  ALU.add).then_inc(x2_ready, 1)

            def chunk(c, prep, layer1):
                for u in range(KT * NQ):
                    k, q = divmod(u, NQ)
                    if layer1 and u in U_PROD:
                        product(c + 1, U_PROD.index(u))
                    if q == Q_SUM and not (k == 0 and isinstance(c, int) and c == 0):
                        sum_tile(c * KT + k - 1, (k - 1) % KT)
                    if WHO[q] == "V":
                        weigh(c, k, q)
                    if layer1 and u == U_X1L:
                        x1_lo_out(c + 1, 0, KT - 1, 1)
                    if u == U_Z1:
                        z1_out(c)
                if layer1:
                    x1_lo_out(c + 1, KT - 1, KT, 2)

            dve.wait_ge(gathered, 16 * M)
            for g in range(0, NG, 2):
                dve.tensor_copy(*first_stage(g)).then_inc(staged0_dve, 1)
            for j in range(NJ):
                product(0, j)
            x1_lo_out(0, 0, KT - 1, 1)
            x1_lo_out(0, KT - 1, KT, 2)
            chunk(0, True, True)
            chunk(1, True, True)
            with dve.Fori(2, NC - NG) as c:
                chunk(c, True, True)
            with dve.Fori(NC - NG, NC - 1) as c:
                chunk(c, False, True)
            chunk(NC - 1, False, False)
            sum_tile(NT - 1, KT - 1)
            dve.wait_ge(dense_out, 2)
            for j in range(1, J1, 2):
                dve.wait_ge(h1_done, j + 1)
                dve.tensor_scalar(h1[:, j * B:(j + 1) * B], h1_bank[j][:, :], b1c[:, j:j + 1], 0.0,
                                  ALU.add, ALU.max).then_inc(h1_dve, 1)
            dve.wait_ge(h2_done, 2)
            dve.tensor_scalar(h2[:, B:2 * B], h2_bank[1][:, :], b2c[:, 1:2], 0.0,
                              ALU.add, ALU.max).then_inc(h2_dve, 1)
            dve.wait_ge(y_done, 1)
            dve.tensor_copy(y_row, g_bank[0:1, 0:B]).then_inc(y_copied, 1)

        @block.tensor
        def _(pe):
            def setup_turn(i):
                kind, g = GROUPS[i]
                if i >= NY:
                    j = i - NY
                    if GROUPS[j][0] == "k1":
                        pe.wait_ge(dve_setup, G_K1.index(j) + 1)
                    else:
                        pe.wait_ge(act_setup, j + 1)
                if kind == "k0":
                    pe.wait_ge(w0_ready, W0_OPS)
                    pe.wait_ge(consts, 1)
                    for b in range(min(4, NJ - 4 * g)):
                        j = 4 * g + b
                        last = pe.transpose(y_bank[i % NY][0:PB, b * H:(b + 1) * H],
                                            w0_pre[:, j * PB:(j + 1) * PB], ident[:, :])
                else:
                    raw, arrived = (k1_raw, k1_in) if kind == "k1" else (k2_raw, k2_in)
                    pe.wait_ge(arrived, 16)
                    for b in range(UM):
                        m = g * UM + b
                        last = pe.transpose(y_bank[i % NY][:, b * H:(b + 1) * H],
                                            raw[:, m:m + (H - 1) * M + 1:M], ident[:, :])
                last.then_inc(turned_k, 1)

            def turn(n):
                if isinstance(n, int) and n < NG:
                    pe.wait_ge((staged0_dve, staged0_act)[n % 2], n // 2 + 1)
                    e = [stage0[:, n * DG + d, :] for d in range(DG)]
                    wait(pe, turn_out, n - 1)
                else:
                    pe.wait_ge(staged, n - NG + 1)
                    e = [stage_v[:, d, :] for d in range(DG)]
                    wait(pe, turn_out, n)
                pe.wait_ge(consts, 1)
                for d in range(DG):
                    last = pe.transpose(turn_bank(n)[0:PB, d * P:(d + 1) * P], e[d], ident[:, :])
                last.then_inc(turned, 1)

            def x0_turn(c):
                pe.wait_ge(base_in, (c + 1) * (16 * SH))
                wait(pe, x0c_ready, c * KT)
                for k in range(KT):
                    last = pe.transpose(ring[1][:, k * PB:(k + 1) * PB], base[:, k * P:(k + 1) * P],
                                        ident[0:PB, 0:PB])
                last.then_inc(x0_turned, 1)

            def fold(c, j):
                pe.wait_ge(prod_done, c * NJ + j + 1)
                if j == 0:
                    wait(pe, x1l_done, 2 * c)
                    wait(pe, z1_done, c)
                b = prod_slot(j)
                pe.matmul(x_bank[:, :], w0_t[:, j * H:(j + 1) * H], prod[0:PB, b * CW:(b + 1) * CW],
                          start=(j == 0), stop=(j == NJ - 1)).then_inc(folded, 1)

            def unit(c, k, q):
                t = c * KT + k
                u = k * NQ + q
                if q == 0:
                    pe.wait_ge(x1l_done, 2 * c + (2 if k == KT - 1 else 1))
                if u >= NY:
                    s, n = freed_by((u - NY) % NQ, c * KT + (u - NY) // NQ)
                else:
                    s, n = freed_by((u - NY) % NQ, (c - 1) * KT + (KT * NQ + u - NY) // NQ)
                wait(pe, s, n)
                bank = y_bank[u % NY][:, :]
                hi, lo = x1_hi[:, k * P:(k + 1) * P], x1_lo[:, k * P:(k + 1) * P]
                s = slice(q * CW, (q + 1) * CW)
                pe.matmul(bank, hi, k1_lo[:, s], start=True, stop=False)
                pe.matmul(bank, hi, k1_hi[:, s], start=False, stop=False)
                pe.matmul(bank, lo, k1_hi[:, s], start=False, stop=True).then_inc(y_ready, 1)

            def g_matmul(t, k):
                par = k % 2
                pe.wait_ge(x2_ready, t + 1)
                pe.wait_ge(diag_ready, t + 1)
                wait(pe, g_out, t)
                pe.matmul(g_bank[:, 0:TB * M1], x2t[:, par * H:(par + 1) * H], diag[:, :],
                          start=True, stop=True).then_inc(g_done, 1)

            def chunk(c, prep, layer1):
                for u in range(KT * NQ):
                    k, q = divmod(u, NQ)
                    for n, u_turn, u_out in preps(c) if prep else ():
                        if u == u_turn:
                            turn(n)
                    if layer1:
                        if u == U_X0T:
                            x0_turn(c + 1)
                        if u in U_FOLD:
                            fold(c + 1, U_FOLD.index(u))
                    if q == Q_G and not (k == 0 and isinstance(c, int) and c == 0):
                        g_matmul(c * KT + k - 1, (k - 1) % KT)
                    unit(c, k, q)

            for i in range(len(GROUPS)):
                setup_turn(i)
            for n in range(NG):
                turn(n)
            x0_turn(0)
            for j in range(NJ):
                fold(0, j)
            pe.wait_ge(act_setup, len(GROUPS))
            pe.wait_ge(dve_setup, NQ)
            chunk(0, True, True)
            chunk(1, True, True)
            with pe.Fori(2, NC - NG) as c:
                chunk(c, True, True)
            with pe.Fori(NC - NG, NC - 1) as c:
                chunk(c, False, True)
            chunk(NC - 1, False, False)
            g_matmul(NT - 1, KT - 1)
            pe.wait_ge(small_in, 64)
            pe.transpose(ring[1][:, 0:J1 + 2 * J2], rows[:, :], ident[0:J1 + 2 * J2, 0:J1 + 2 * J2])
            for t in range(NBT):
                last = pe.transpose(ring[0][0:ND, t * P:(t + 1) * P], dense[:, t * ND:(t + 1) * ND], ident[:, :])
            last.then_inc(dense_done, 1)
            pe.wait_ge(g_out, NT)
            pe.wait_ge(a_unit, NT * NA)
            pe.wait_ge(v_step, NT * VS)
            for m in range(M):
                last = pe.matmul(y_bank[0][:, :], k2_t[:, m * H:(m + 1) * H], G[:, m, :],
                                 start=(m == 0), stop=(m == M - 1))
            last.then_inc(z3_done, 1)
            pe.wait_ge(w_in, 32)
            pe.wait_ge(dense_out, 2)
            pe.wait_ge(z1_done, NC)
            for j in range(J1):
                s = slice(j * P, (j + 1) * P)
                pe.matmul(h1_bank[j][:, :], w1[:, s], z1[:, :], start=True, stop=False)
                pe.matmul(h1_bank[j][:, :], w1[:, N1 + j * P:N1 + (j + 1) * P], G[:, M, :], start=False, stop=False)
                pe.matmul(h1_bank[j][:, :], w1d[:, s], dense_t, start=False, stop=False)
            pe.wait_ge(z3_out, 1)
            for j in range(J1):
                pe.matmul(h1_bank[j][:, :], w1[:, 2 * N1 + j * P:2 * N1 + (j + 1) * P], z3,
                          start=False, stop=True).then_inc(h1_done, 1)
            pe.wait_ge(w2_in, 16)
            for i in range(J2):
                for j in range(J1):
                    if i == 0:
                        pe.wait_ge(*((h1_act, j // 2 + 1) if j % 2 == 0 else (h1_dve, j // 2 + 1)))
                    last = pe.matmul(h2_bank[i][:, :], w2[:, j * N2 + i * P:j * N2 + (i + 1) * P],
                                     h1[:, j * B:(j + 1) * B], start=(j == 0), stop=(j == J1 - 1))
                last.then_inc(h2_done, 1)
            pe.wait_ge(h2_act, 1)
            pe.matmul(g_bank[0:1, 0:B], w3c[:, 0:1], h2[:, 0:B], start=True, stop=False)
            pe.wait_ge(h2_dve, 1)
            pe.matmul(g_bank[0:1, 0:B], w3c[:, 1:2], h2[:, B:2 * B], start=False, stop=True).then_inc(y_done, 1)


N_TABLES = 40
_INS = ["dense_ctx", "ids"] + [f"tbl_{i}" for i in range(N_TABLES)] + \
       ["W_top1", "b_top1", "W_top2", "b_top2", "W_top3", "L0_rec_k0", "L0_rec_k1", "L0_rec_k2"]


def kernel(**inputs):
    import numpy as _np
    import concourse.bacc as _bacc
    from concourse import mybir as _mybir
    from concourse.bass_utils import run_bass_kernel_spmd as _run

    nc = _bacc.Bacc("TRN2", target_bir_lowering=False, num_devices=1)
    arrays, aps = {}, {}
    for name in _INS:
        a = _np.ascontiguousarray(inputs[name])
        arrays[f"in_{name}_dram"] = a
        aps[name] = nc.dram_tensor(f"in_{name}_dram", a.shape, _mybir.dt.from_np(a.dtype), kind="ExternalInput").ap()
    out = nc.dram_tensor("out_0_dram", (aps["ids"].shape[0], 1), _mybir.dt.float32, kind="ExternalOutput").ap()
    cin_tower(nc, aps["dense_ctx"], aps["ids"], [aps[f"tbl_{i}"] for i in range(N_TABLES)],
              aps["W_top1"], aps["b_top1"], aps["W_top2"], aps["b_top2"], aps["W_top3"],
              aps["L0_rec_k0"], aps["L0_rec_k1"], aps["L0_rec_k2"], out)
    r = _run(nc, [arrays], core_ids=[0])
    return r.results[0]["out_0_dram"]
```

```python
import concourse.bass as bass
from concourse import mybir
from contextlib import ExitStack



def cin_tower(nc, dense_ctx, ids, tables, W_top1, b_top1, W_top2, b_top2, W_top3, k0, k1, k2, out):
    fp32 = mybir.dt.float32
    fp32r = mybir.dt.float32r
    i32 = mybir.dt.int32
    u32 = mybir.dt.uint32
    ALU = mybir.AluOpType
    ACT = mybir.ActivationFunctionType
    AX = mybir.AxisListType

    B, M = ids.shape
    D = tables[0].shape[1]
    H = k1.shape[0]
    P = 128
    NBT = B // P
    CB = 32
    CW = CB * D
    NC = B // CB
    TB = P // D
    KT = CW // P
    NT = NC * KT
    SH = 3
    PB = SH * M
    NJ = (M // 2 + 1) // SH
    NS = NJ * SH
    UM = CW // H
    NQ = M // UM
    M1 = M + 1
    DG = 4
    NG = D // DG
    N1, N2 = W_top1.shape[1], W_top2.shape[1]
    J1, J2 = N1 // P, N2 // P
    ND = dense_ctx.shape[1]

    LATE = 8
    WHO = [["VAVAVVAVAV", "VAVAVVAVAV", "VAVAVVAVAV", "VAVAVVAVAV"],
           ["AVAVAVAVAV", "AVAVAAVAVA", "AVAAVVAVAV", "VAVAVVAVAV"]]
    NZ = 4
    NY = 5
    NP = 2
    NR = 2
    EARLY = 25
    GATHER_TILES = [5, 11, 16]

    U_TURN, U_TURNED = 5, 6
    U_TURN_1, U_TURNED_1 = [24, 32], [26, 34]
    U_X0T = 28
    U_PROD = [10, 12, 15, 18, 21, 22, 28]
    U_FOLD = [u + 5 for u in U_PROD]
    U_Z1 = 7
    U_X1H, U_X1L = 33, 34
    U_DENSE, U_DENSED = 31, 33
    Q_SUM, Q_G, Q_GOUT = 3, 8, 9
    Q_X0C = 4

    ctx = ExitStack()
    with ctx:
        def sb(name, shape, dt=fp32):
            return ctx.enter_context(nc.sbuf_tensor(name, shape, dt))

        def sem(name):
            return ctx.enter_context(nc.semaphore(name))

        region = sb("region", [P, M1 * B])
        G = region[:, :].rearrange("p (m b) -> p m b", m=M1)
        at = [0]

        def carve(n):
            at[0] += n
            assert at[0] <= M1 * B
            return region[:, at[0] - n:at[0]]
        k0_raw = carve(M * M)
        k1_raw = carve(H * M)
        k2_raw = carve(H * M)
        w0_pre = carve(NS * M)

        k1_hi = sb("k1_hi", [P, M * H], fp32r)
        k1_lo = sb("k1_lo", [P, M * H], fp32r)
        k2_t = sb("k2_t", [P, M * H])
        w0_t = sb("w0_t", [PB, NJ * H])
        ident = sb("ident", [P, P])
        row_mask = sb("row_mask", [P, TB])
        idx = sb("idx", [P, NBT * M], i32)
        emb = sb("emb", [P, M * NBT * D])
        stage = sb("stage", [P, DG * PB])
        et = sb("et", [PB, 2 * P * D])
        shift = sb("shift", [PB, NR * CW])
        base = sb("base", [PB, CW])
        prod = sb("prod", [P, NP * CW])
        x0c = sb("x0c", [P, 2 * M1])
        x1_hi = sb("x1_hi", [P, CW], fp32r)
        x1_lo = sb("x1_lo", [P, CW], fp32r)
        acc = sb("acc", [P, 2 * 2 * H])
        x2t = sb("x2t", [P, 2 * H])
        zw = sb("zw", [P, NZ * CW])
        psum4 = sb("psum4", [P, CW])
        pacc = sb("pacc", [P, 2 * 2 * H])
        diag = sb("diag", [P, TB * M1])
        z1 = sb("z1", [P, B])
        cols = sb("cols", [P, J1 + 2 * J2])
        b1c, b2c, w3c = cols[:, 0:J1], cols[:, J1:J1 + J2], cols[:, J1 + J2:]
        dense_t = base[0:ND, 0:B]
        w1 = emb[:, 0:3 * N1]
        w1d = emb[0:ND, 3 * N1:4 * N1]
        dense = emb[:, 4 * N1:4 * N1 + NBT * ND]
        rows = emb[0:J1 + 2 * J2, 4 * N1 + NBT * ND:4 * N1 + NBT * ND + P]
        h1 = zw[:, 0:J1 * B]
        stage0 = zw[:, 0:D * PB].rearrange("p (d f) -> p d f", d=D)
        z3 = prod[:, 0:B]
        h2 = k2_t[:, 0:J2 * B]
        w2 = k2_t[:, J2 * B:J2 * B + J1 * N2]
        y_row = acc[0:1, 0:B]

        y_bank = [ctx.enter_context(nc.psum_tensor(f"y_bank{i}", [P, CW], fp32)) for i in range(NY)]
        e_bank = ctx.enter_context(nc.psum_tensor("e_bank", [P, CW], fp32))
        x_bank = ctx.enter_context(nc.psum_tensor("x_bank", [P, CW], fp32))
        g_bank = ctx.enter_context(nc.psum_tensor("g_bank", [P, CW], fp32))
        assert TB * M1 + KT * M <= CW
        x0_turned_e = g_bank[:, TB * M1:TB * M1 + KT * M]

        ids_in = sem("ids_in")
        k0_in, k1_in, k2_in = sem("k0_in"), sem("k1_in"), sem("k2_in")
        small_in = sem("small_in")
        w_in, w2_in = sem("w_in"), sem("w2_in")
        gathered = sem("gathered")
        consts = sem("consts")
        const_step = sem("const_step")
        ROW_MASK = 4
        w0_ready = sem("w0_ready")
        turned_k = sem("turned_k")
        act_setup, dve_setup = sem("act_setup"), sem("dve_setup")
        ones_ready = sem("ones_ready")
        staged0_dve, staged0_act, staged = sem("staged0_dve"), sem("staged0_act"), sem("staged")
        turned, turn_out = sem("turned"), sem("turn_out")
        base_in = sem("base_in")
        shift_in = [sem(f"shift_in{i}") for i in range(NR)]
        first_in = [sem(f"first_in{i}") for i in range(NJ - 1 - NR)]
        prod_done = sem("prod_done")
        x0_turned = sem("x0_turned")
        folded = sem("folded")
        x1h_done, x1l_done, z1_done = sem("x1h_done"), sem("x1l_done"), sem("z1_done")
        y_ready = sem("y_ready")
        v_step, a_unit, p_add = sem("v_step"), sem("a_unit"), sem("p_add")
        x0c_ready, diag_ready = sem("x0c_ready"), sem("diag_ready")
        sum_half, x2_ready = sem("sum_half"), sem("x2_ready")
        g_done, g_out = sem("g_done"), sem("g_out")
        k2_hi_done, k2_lo_done = sem("k2_hi_done"), sem("k2_lo_done")
        g_hi_done, g_lo_done, z3_step = sem("g_hi_done"), sem("g_lo_done"), sem("z3_step")
        z3_out = sem("z3_out")
        dense_done, dense_out = sem("dense_done"), sem("dense_out")
        h1_done, h1_act, h1_dve = sem("h1_done"), sem("h1_act"), sem("h1_dve")
        h2_done, h2_act, h2_dve = sem("h2_done"), sem("h2_act"), sem("h2_dve")
        y_done, y_copied, y_stored = sem("y_done"), sem("y_copied"), sem("y_stored")

        def wait(eng, s, n):
            if isinstance(n, int) and n <= 0:
                return
            eng.wait_ge(s, n)

        assert WHO[0][-1] == WHO[1][-1]

        def units(kind, late, k):
            return [q for q in range(NQ) if WHO[late][k][q] == kind]

        def before(kind, c, k, late):
            per = [sum(len(units(kind, i, kk)) for kk in range(KT)) for i in range(2)]
            tiles = range(k) if k >= 0 else range(k, 0)
            part = sum(len(units(kind, late, kk)) for kk in tiles)
            return c * per[late] + late * LATE * (per[0] - per[1]) + (part if k >= 0 else -part)

        def v_steps(c, k, late):
            return UM * before("V", c, k, late)

        def a_units(c, k, late):
            return before("A", c, k, late)

        def adds(c, k, late):
            return before("A", c, k, late)

        def freed_by(q, c, k, late):
            if q in units("V", late, k):
                return v_step, v_steps(c, k, late) + UM * (units("V", late, k).index(q) + 1)
            return a_unit, a_units(c, k, late) + units("A", late, k).index(q) + 1

        def zw_slot(late, k, a):
            s = (sum(len(units("A", late, kk)) for kk in range(k)) + a) % NZ
            return zw[:, s * CW:(s + 1) * CW]
        for late in range(2):
            assert sum(len(units("A", late, k)) for k in range(KT)) % NZ == 0

        W0_OPS = sum(len({0, s % SH, (s % SH - s) % M, M}) - 1 for s in range(NS))
        GROUPS = [("k0", g) for g in range(-(-NJ // 4))] + [("k1", g) for g in range(NQ)] + \
                 [("k2", g) for g in range(NQ)]
        G_K1 = [i for i, g in enumerate(GROUPS) if g[0] == "k1"]

        def emb_step(n):
            return emb[:, :].rearrange("p (f r) -> p f r", f=M)[:, :, bass.ds(n * DG, DG)].rearrange("p f d -> p d f")

        def prod_slot(j):
            return j % NP

        PER_SLOT = (NJ - 1) // NR
        assert PER_SLOT * NR == NJ - 1 and (NJ - 1 - NR) % NR == 0 and NJ - 1 - NR <= NZ

        FIRST = NJ - 1 - NR
        first_shift = [zw[0:PB, i * CW:(i + 1) * CW] for i in range(FIRST)]

        def shift_slot(j):
            return (j - 1) % NR

        def shifted(c, j):
            if isinstance(c, int) and c == 0 and j <= FIRST:
                return first_shift[j - 1], first_in[j - 1]
            b = shift_slot(j)
            return shift[:, b * CW:(b + 1) * CW], shift_in[b]

        def shift_value(c, j):
            if isinstance(c, int) and c == 0 and j <= FIRST:
                return 16 * 2
            return (c * PER_SLOT + (j - 1) // NR + 1 - FIRST // NR) * (16 * 2)

        def e_columns(c):
            return et[:, bass.ds((c % (2 * KT)) * CW, CW)]

        NK2 = NQ // 2

        def k2_slot(g):
            return slice(g % NK2 * CW, (g % NK2 + 1) * CW)
        NG3 = NQ - NK2
        G_hi, G_lo = ([half[:, (NK2 + i) * CW:(NK2 + i) * CW + B] for i in range(NG3)] for half in (k1_hi, k1_lo))
        h1_bank = [x_bank, e_bank, y_bank[1], y_bank[2]]
        h2_bank = [y_bank[3], y_bank[4]]
        emb_tile0 = emb[:, :].rearrange("p (f r) -> p f r", f=M)[:, :, 0:D].rearrange("p f d -> p d f")
        stage_v = stage[:, :].rearrange("p (d f) -> p d f", d=DG)

        def thrice(v):
            return v.rearrange("p d (n f) -> p n d f", n=SH)

        def first_stage(g):
            d = slice(g * DG, (g + 1) * DG)
            return thrice(stage0[:, d, :]), emb_tile0[:, d, :].unsqueeze(1).broadcast_to([P, SH, DG, M])

        def turn_bank(n):
            return (e_bank, x_bank)[n % 2] if isinstance(n, int) and n < NG else e_bank

        def preps(c):
            if not isinstance(c, int):
                return [(c + NG, U_TURN, U_TURNED)]
            if c == 1:
                return [(NG + i, U_TURN_1[i], U_TURNED_1[i]) for i in range(2)]
            return []

        block = ctx.enter_context(nc.Block())

        @block.sync
        def _(sp):
            sp.dma_start(idx[:, :].rearrange("p (t f) -> p t f", t=NBT),
                         ids.rearrange("(t p) f -> p t f", p=P)).then_inc(ids_in, 16)
            sp.dma_start(k0_raw, k0.rearrange("o h m -> o (h m)")).then_inc(k0_in, 16)
            sp.dma_start(k1_raw, k1.rearrange("o h m -> o (h m)")).then_inc(k1_in, 16)
            sp.dma_start(k2_raw, k2.rearrange("o h m -> o (h m)")).then_inc(k2_in, 16)

            def copy_rows(dst, first, n, row, column, done):
                sp.dma_start(dst[first:first + n, :], et[row:row + n, bass.ds(column, CW)]).then_inc(done, 16)

            def spread(c):
                column = (c % (2 * KT)) * CW
                if not isinstance(c, int):
                    column = sp.snap(column)
                wait(sp, prod_done, c * NJ)
                sp.wait_ge(turn_out, (c // KT + 1) * NG)
                wait(sp, x0_turned, c)
                for n in range(SH):
                    copy_rows(base[:, :], n * M, M, (M - n) % M, column, base_in)
                for j in range(1, NJ):
                    to, done = shifted(c, j)
                    if j > NR and not (isinstance(c, int) and c == 0):
                        sp.wait_ge(prod_done, c * NJ + j - NR + 1)
                    copy_rows(to, 0, PB - SH * j, SH * j, column, done)
                    copy_rows(to, PB - SH * j, SH * j, 0, column, done)

            spread(0)
            spread(1)
            with sp.Fori(2, NC) as c:
                spread(c)
            sp.wait_ge(staged, NC - NG)
            sp.dma_start(rows[0:J1, :], b_top1.rearrange("(j p) -> j p", p=P)).then_inc(small_in, 16)
            sp.dma_start(rows[J1:J1 + J2, :], b_top2.rearrange("(j p) -> j p", p=P)).then_inc(small_in, 16)
            sp.dma_start(rows[J1 + J2:J1 + 2 * J2, :],
                         W_top3.rearrange("(j p) n -> j (p n)", p=P)).then_inc(small_in, 16)
            sp.dma_start(dense.rearrange("p (t n) -> p t n", t=NBT),
                         dense_ctx.rearrange("(t p) n -> p t n", p=P)).then_inc(small_in, 16)
            sp.dma_start(w1.rearrange("p (j n) -> p j n", j=3),
                         W_top1[0:3 * H, :].rearrange("(j p) n -> p j n", p=P)).then_inc(w_in, 16)
            sp.dma_start(w1d, W_top1[3 * H:3 * H + ND, :]).then_inc(w_in, 16)
            sp.wait_ge(k2_lo_done, NQ)
            sp.dma_start(w2.rearrange("p (j n) -> p j n", j=J1),
                         W_top2.rearrange("(j p) n -> p j n", p=P)).then_inc(w2_in, 16)
            sp.wait_ge(y_copied, 1)
            sp.dma_start(out.rearrange("b n -> n b"), y_row).then_inc(y_stored, 16)
            sp.wait_ge(y_stored, 16)

        @block.gpsimd
        def _(pool):
            pool.memset(ident[:, :], 0.0).then_inc(const_step, 1)
            pool.wait_ge(const_step, 1)
            pool.affine_select(out=ident[:, :], in_=ident[:, :], compare_op=ALU.not_equal, fill=1.0,
                               base=0, pattern=[[-1, P]], channel_multiplier=1).then_inc(consts, 1)

            def gather(t, features):
                if 0 in features:
                    wait(pool, gathered, 16 * M * t)
                for f in features:
                    a = (f * NBT + t) * D
                    pool.indirect_dma_start(
                        out=emb[:, a:a + D], out_offset=None, in_=tables[f],
                        in_offset=bass.IndirectOffsetOnAxis(
                            ap=idx[:, t * M + f:t * M + f + 1].bitcast(u32), axis=0),
                    ).then_inc(gathered, 16)

            pool.wait_ge(ids_in, 16)
            gather(0, range(M))

            pool.memset(row_mask[:, :], 1.0).then_inc(const_step, 1)
            pool.wait_ge(const_step, 2)
            pool.affine_select(out=row_mask[:, :], in_=row_mask[:, :], compare_op=ALU.is_ge, fill=0.0,
                               base=0, pattern=[[-D, TB]], channel_multiplier=1).then_inc(const_step, 1)
            pool.wait_ge(const_step, 3)
            pool.affine_select(out=row_mask[:, :], in_=row_mask[:, :], compare_op=ALU.is_ge, fill=0.0,
                               base=D - 1, pattern=[[D, TB]], channel_multiplier=-1).then_inc(const_step, 1)
            gather(1, range(EARLY))

            def add_units(c, k, late):
                t = c * KT + k
                done, n = adds(c, k, late), len(units("A", late, k))
                for a in range(1, n):
                    pool.wait_ge(a_unit, a_units(c, k, late) + a + 1)
                    if a == 1:
                        one = zw_slot(late, k, 0)
                        wait(pool, p_add, done)
                    else:
                        one = psum4[:, :]
                        pool.wait_ge(p_add, done + a - 1)
                    pool.tensor_tensor(psum4[:, :], one, zw_slot(late, k, a), ALU.add).then_inc(p_add, 1)
                pool.wait_ge(p_add, done + n - 1)
                wait(pool, x2_ready, t - 1)
                par = k % 2
                pool.tensor_tensor(pacc[:, par * 2 * H:(par + 1) * 2 * H], psum4[:, 0:2 * H], psum4[:, 2 * H:4 * H],
                                   ALU.add).then_inc(p_add, 1)

            def diagonal(c, k):
                t = c * KT + k
                pool.wait_ge(x0c_ready, t + 1)
                wait(pool, g_done, t)
                if isinstance(c, int) and t == 0:
                    pool.wait_ge(const_step, ROW_MASK)
                par = k % 2
                shape = [P, TB, M1]
                pool.tensor_tensor(
                    diag[:, :].rearrange("p (b m) -> p b m", b=TB),
                    x0c[:, par * M1:(par + 1) * M1].unsqueeze(1).broadcast_to(shape),
                    row_mask[:, :].unsqueeze(2).broadcast_to(shape), ALU.mult).then_inc(diag_ready, 1)

            def chunk(c, late, gathers=()):
                for k in range(KT):
                    for part in gathers[k:k + 1]:
                        gather(*part)
                    add_units(c, k, late)
                    diagonal(c, k)

            part_of = []
            for t, tiles in zip(range(1, NBT), GATHER_TILES):
                first = EARLY if t == 1 else 0
                cut_at = [first + (M - first) * i // tiles for i in range(tiles + 1)]
                part_of += [(t, range(cut_at[i], cut_at[i + 1])) for i in range(tiles)]
            assert len(part_of) == LATE * KT
            for c in range(LATE):
                chunk(c, 0, part_of[c * KT:(c + 1) * KT])
            with pool.Fori(LATE, NC) as c:
                chunk(c, 1)
            pool.wait_ge(y_ready, NT * NQ)
            for g in range(NQ):
                pool.wait_ge(k2_hi_done, g + 1)
                pool.tensor_tensor(k1_lo[:, k2_slot(g)], k2_t[:, g * CW:(g + 1) * CW],
                                   k1_hi[:, k2_slot(g)].bitcast(fp32), ALU.subtract).then_inc(k2_lo_done, 1)

        @block.scalar
        def _(act):
            def setup_out(i):
                kind, g = GROUPS[i]
                act.wait_ge(turned_k, i + 1)
                src = y_bank[i % NY]
                if kind == "k0":
                    n = min(4, NJ - 4 * g) * H
                    act.activation(w0_t[:, 4 * g * H:4 * g * H + n], src[0:PB, 0:n], ACT.Copy).then_inc(act_setup, 1)
                elif kind == "k1":
                    act.activation(k1_hi[:, g * CW:(g + 1) * CW], src[:, :], ACT.Copy).then_inc(act_setup, 1)
                else:
                    act.activation(k2_t[:, g * CW:(g + 1) * CW], src[:, :], ACT.Copy).then_inc(act_setup, 1)

            def stage_e(n):
                act.wait_ge(gathered, (n // NG + 1) * (16 * M))
                wait(act, turned, n)
                e = emb_step(n)
                act.activation(thrice(stage_v), e.unsqueeze(1).broadcast_to([P, SH, DG, M]), ACT.Copy).then_inc(staged, 1)

            def turn_evac(n, c):
                act.wait_ge(turned, n + 1)
                wait(act, prod_done, c * NJ)
                v = et[:, :].rearrange("p (r b g e) -> p r g b e", r=2, b=P, g=NG)
                act.activation(v[:, (n // NG) % 2, n % NG, :, :],
                               turn_bank(n)[0:PB, :].rearrange("p (e b) -> p b e", e=DG),
                               ACT.Copy).then_inc(turn_out, 1)

            def x0c_copy(c, k, late):
                t = c * KT + k
                act.wait_ge(x0_turned, c + 1)
                if isinstance(c, int) and c + k == 0:
                    act.wait_ge(ones_ready, 1)
                wait(act, v_step, v_steps(c, k - 1, late))
                wait(act, diag_ready, t - 1)
                par = k % 2
                act.activation(x0c[:, par * M1:par * M1 + M], x0_turned_e[:, k * M:(k + 1) * M], ACT.Copy).then_inc(x0c_ready, 1)

            def x1_hi_out(c, k0_, k1_):
                act.wait_ge(folded, NJ * (c + 1))
                wait(act, y_ready, ((c - 1) * KT + k1_) * NQ)
                if k0_:
                    act.wait_ge(x1l_done, 2 * c + 1)
                s = slice(k0_ * P, k1_ * P)
                act.activation(x1_hi[:, s], x_bank[:, s], ACT.Copy).then_inc(x1h_done, 1)

            def weigh(c, k, q, late):
                t = c * KT + k
                a = units("A", late, k).index(q)
                act.wait_ge(y_ready, t * NQ + q + 1)
                if a == 0:
                    act.wait_ge(x0c_ready, t + 1)
                kk, aa = k, a - NZ
                while aa < 0:
                    kk -= 1
                    aa += len(units("A", late, kk))
                wait(act, p_add, adds(c, kk, late) + max(aa, 1))
                z = zw_slot(late, k, a)
                par = k % 2
                for i in range(UM):
                    m = q * UM + i
                    last = act.activation(z[:, i * H:(i + 1) * H],
                                          y_bank[(k * NQ + q) % NY][:, i * H:(i + 1) * H], ACT.Copy,
                                          scale=x0c[:, par * M1 + m:par * M1 + m + 1])
                last.then_inc(a_unit, 1)

            def g_evac(t):
                act.wait_ge(g_done, t + 1)
                act.activation(G[:, :, bass.ds(t * TB, TB)],
                               g_bank[:, 0:TB * M1].rearrange("p (b m) -> p m b", b=TB),
                               ACT.Copy).then_inc(g_out, 1)

            def dense_evac():
                act.wait_ge(dense_done, 1)
                act.activation(dense_t, e_bank[0:ND, 0:B], ACT.Copy).then_inc(dense_out, 1)
                act.activation(cols[:, :], x_bank[:, 0:J1 + 2 * J2], ACT.Copy).then_inc(dense_out, 1)

            def chunk(c, late, prep=True, layer1=True):
                for u in range(KT * NQ):
                    k, q = divmod(u, NQ)
                    if not layer1 and u == U_DENSED:
                        dense_evac()
                    for n, u_turn, u_out in preps(c) if prep else ():
                        if u == u_turn - 3:
                            stage_e(n)
                        if u == u_out:
                            turn_evac(n, c)
                    if q == Q_X0C:
                        if k < KT - 1:
                            x0c_copy(c, k + 1, late)
                        elif layer1:
                            x0c_copy(c + 1, 0, late)
                    if q == Q_GOUT and not (k == 0 and isinstance(c, int) and c == 0):
                        g_evac(c * KT + k - 1)
                    if WHO[late][k][q] == "A":
                        weigh(c, k, q, late)
                    if layer1 and u == U_X1H:
                        x1_hi_out(c + 1, 0, KT - 1)
                if layer1:
                    x1_hi_out(c + 1, KT - 1, KT)

            for i in range(len(GROUPS)):
                setup_out(i)
            act.wait_ge(gathered, 16 * M)
            for g in range(1, NG, 2):
                act.activation(*first_stage(g), ACT.Copy).then_inc(staged0_act, 1)
            for n in range(NG):
                turn_evac(n, 0)
            x0c_copy(0, 0, 0)
            x1_hi_out(0, 0, KT - 1)
            x1_hi_out(0, KT - 1, KT)
            chunk(0, 0)
            chunk(1, 0)
            with act.Fori(2, LATE) as c:
                chunk(c, 0)
            with act.Fori(LATE, NC - NG) as c:
                chunk(c, 1)
            with act.Fori(NC - NG, NC - 1) as c:
                chunk(c, 1, prep=False)
            chunk(NC - 1, 1, prep=False, layer1=False)
            act.wait_ge(y_ready, NT * NQ)

            def k2_hi_out(g):
                wait(act, z3_step, UM * (g - NK2 + 1))
                act.activation(k1_hi[:, k2_slot(g)], k2_t[:, g * CW:(g + 1) * CW], ACT.Copy).then_inc(k2_hi_done, 1)

            for g in range(NK2):
                k2_hi_out(g)
            g_evac(NT - 1)
            act.wait_ge(g_out, NT)
            for m in range(M):
                if m % UM == UM - 1 and NK2 <= NK2 + m // UM - 1 < NQ:
                    k2_hi_out(NK2 + m // UM - 1)
                wait(act, z3_step, m - NG3 + 1)
                act.activation(G_hi[m % NG3], G[:, m, :], ACT.Copy).then_inc(g_hi_done, 1)
            act.wait_ge(dense_out, 2)
            act.wait_ge(z3_step, M)
            act.activation(z3, y_bank[0][:, :], ACT.Copy).then_inc(z3_out, 1)
            for j in range(0, J1, 2):
                act.wait_ge(h1_done, j + 1)
                act.activation(h1[:, j * B:(j + 1) * B], h1_bank[j][:, :], ACT.Relu,
                               bias=b1c[:, j:j + 1]).then_inc(h1_act, 1)
            act.wait_ge(h2_done, 1)
            act.activation(h2[:, 0:B], h2_bank[0][:, :], ACT.Relu, bias=b2c[:, 0:1]).then_inc(h2_act, 1)

        @block.vector
        def _(dve):
            dve.memset(x0c[:, :], 1.0).then_inc(ones_ready, 1)
            dve.wait_ge(k0_in, 16)
            for s in range(NS):
                n = s % SH
                ends = sorted({0, n, (n - s) % M, M})
                for lo, hi in zip(ends, ends[1:]):
                    i, j = (lo - n) % M, (lo - n + s) % M
                    dst = w0_pre[:, s * M + lo:s * M + hi]
                    one, two = (k0_raw[:, a:a + (hi - lo - 1) * (M + 1) + 1:M + 1] for a in (i * M + j, j * M + i))
                    if s == 0 or 2 * s == M:
                        dve.tensor_copy(dst, one).then_inc(w0_ready, 1)
                    else:
                        dve.tensor_tensor(dst, one, two, ALU.add).then_inc(w0_ready, 1)
            for i in G_K1:
                g = GROUPS[i][1]
                dve.wait_ge(act_setup, i + 1)
                s = slice(g * CW, (g + 1) * CW)
                dve.tensor_tensor(k1_lo[:, s], y_bank[i % NY][:, :], k1_hi[:, s].bitcast(fp32),
                                  ALU.subtract).then_inc(dve_setup, 1)

            def product(c, j):
                if j == 0:
                    dve.wait_ge(base_in, (c + 1) * (16 * SH))
                    other = e_columns(c)
                else:
                    other, arrived = shifted(c, j)
                    dve.wait_ge(arrived, shift_value(c, j))
                wait(dve, folded, c * NJ + j - NP + 1)
                b = prod_slot(j)
                dve.tensor_tensor(prod[0:PB, b * CW:(b + 1) * CW], base[:, :], other,
                                  ALU.mult).then_inc(prod_done, 1)

            def x1_lo_out(c, k0_, k1_, n):
                dve.wait_ge(x1h_done, 2 * c + n)
                s = slice(k0_ * P, k1_ * P)
                dve.tensor_tensor(x1_lo[:, s], x_bank[:, s], x1_hi[:, s].bitcast(fp32),
                                  ALU.subtract).then_inc(x1l_done, 1)

            def z1_out(c):
                dve.tensor_reduce(z1[:, bass.ds(c * CB, CB)], x_bank[:, :].rearrange("p (b d) -> p b d", b=CB),
                                  AX.X, ALU.add).then_inc(z1_done, 1)

            def weigh(c, k, q, late):
                t = c * KT + k
                v = units("V", late, k).index(q)
                par = k % 2
                dve.wait_ge(y_ready, t * NQ + q + 1)
                if v == 0:
                    dve.wait_ge(x0c_ready, t + 1)
                    wait(dve, x2_ready, t - 1)
                for i in range(UM):
                    n = v * UM + i
                    m = q * UM + i
                    a = acc[:, (2 * par + n % 2) * H:(2 * par + n % 2 + 1) * H]
                    y = y_bank[(k * NQ + q) % NY][:, i * H:(i + 1) * H]
                    e = x0c[:, par * M1 + m:par * M1 + m + 1]
                    if n < 2:
                        dve.tensor_scalar(a, y, e, None, ALU.mult).then_inc(v_step, 1)
                    else:
                        dve.wait_ge(v_step, v_steps(c, k, late) + n - 1)
                        dve.scalar_tensor_tensor(out=a, in0=y, scalar=e, in1=a, op0=ALU.mult,
                                                 op1=ALU.add).then_inc(v_step, 1)

            def sum_tile(c, k, late):
                t, par = c * KT + k, k % 2
                dve.wait_ge(v_step, v_steps(c, k + 1, late))
                dve.wait_ge(p_add, adds(c, k + 1, late))
                both = slice(par * 2 * H, (par + 1) * 2 * H)
                dve.tensor_tensor(acc[:, both], acc[:, both], pacc[:, both], ALU.add).then_inc(sum_half, 1)
                dve.wait_ge(sum_half, t + 1)
                wait(dve, g_done, t - 1)
                one, two = (acc[:, (2 * par + i) * H:(2 * par + i + 1) * H] for i in range(2))
                dve.tensor_tensor(x2t[:, par * H:(par + 1) * H], one, two, ALU.add).then_inc(x2_ready, 1)

            def chunk(c, late, prep=True, layer1=True):
                for u in range(KT * NQ):
                    k, q = divmod(u, NQ)
                    if layer1 and u in U_PROD:
                        product(c + 1, U_PROD.index(u))
                    if q == Q_SUM and not (k == 0 and isinstance(c, int) and c == 0):
                        sum_tile(c, k - 1, late)
                    if WHO[late][k][q] == "V":
                        weigh(c, k, q, late)
                    if layer1 and u == U_X1L:
                        x1_lo_out(c + 1, 0, KT - 1, 1)
                    if u == U_Z1:
                        z1_out(c)
                if layer1:
                    x1_lo_out(c + 1, KT - 1, KT, 2)

            dve.wait_ge(gathered, 16 * M)
            for g in range(0, NG, 2):
                dve.tensor_copy(*first_stage(g)).then_inc(staged0_dve, 1)
            for j in range(NJ):
                product(0, j)
            x1_lo_out(0, 0, KT - 1, 1)
            x1_lo_out(0, KT - 1, KT, 2)
            chunk(0, 0)
            chunk(1, 0)
            with dve.Fori(2, LATE) as c:
                chunk(c, 0)
            with dve.Fori(LATE, NC - NG) as c:
                chunk(c, 1)
            with dve.Fori(NC - NG, NC - 1) as c:
                chunk(c, 1, prep=False)
            chunk(NC - 1, 1, prep=False, layer1=False)
            sum_tile(NC - 1, KT - 1, 1)
            for m in range(M):
                dve.wait_ge(g_hi_done, m + 1)
                dve.tensor_tensor(G_lo[m % NG3], G[:, m, :], G_hi[m % NG3].bitcast(fp32),
                                  ALU.subtract).then_inc(g_lo_done, 1)
            dve.wait_ge(dense_out, 2)
            for j in range(1, J1, 2):
                dve.wait_ge(h1_done, j + 1)
                dve.tensor_scalar(h1[:, j * B:(j + 1) * B], h1_bank[j][:, :], b1c[:, j:j + 1], 0.0,
                                  ALU.add, ALU.max).then_inc(h1_dve, 1)
            dve.wait_ge(h2_done, 2)
            dve.tensor_scalar(h2[:, B:2 * B], h2_bank[1][:, :], b2c[:, 1:2], 0.0,
                              ALU.add, ALU.max).then_inc(h2_dve, 1)
            dve.wait_ge(y_done, 1)
            dve.tensor_copy(y_row, g_bank[0:1, 0:B]).then_inc(y_copied, 1)

        @block.tensor
        def _(pe):
            def setup_turn(i):
                kind, g = GROUPS[i]
                if i >= NY:
                    j = i - NY
                    if GROUPS[j][0] == "k1":
                        pe.wait_ge(dve_setup, G_K1.index(j) + 1)
                    else:
                        pe.wait_ge(act_setup, j + 1)
                if kind == "k0":
                    pe.wait_ge(w0_ready, W0_OPS)
                    pe.wait_ge(consts, 1)
                    for b in range(min(4, NJ - 4 * g)):
                        j = 4 * g + b
                        last = pe.transpose(y_bank[i % NY][0:PB, b * H:(b + 1) * H],
                                            w0_pre[:, j * PB:(j + 1) * PB], ident[:, :])
                else:
                    raw, arrived = (k1_raw, k1_in) if kind == "k1" else (k2_raw, k2_in)
                    pe.wait_ge(arrived, 16)
                    for b in range(UM):
                        m = g * UM + b
                        last = pe.transpose(y_bank[i % NY][:, b * H:(b + 1) * H],
                                            raw[:, m:m + (H - 1) * M + 1:M], ident[:, :])
                last.then_inc(turned_k, 1)

            def turn(n):
                if isinstance(n, int) and n < NG:
                    pe.wait_ge((staged0_dve, staged0_act)[n % 2], n // 2 + 1)
                    e = [stage0[:, n * DG + d, :] for d in range(DG)]
                    wait(pe, turn_out, n - 1)
                else:
                    pe.wait_ge(staged, n - NG + 1)
                    e = [stage_v[:, d, :] for d in range(DG)]
                    wait(pe, turn_out, n)
                pe.wait_ge(consts, 1)
                for d in range(DG):
                    last = pe.transpose(turn_bank(n)[0:PB, d * P:(d + 1) * P], e[d], ident[:, :])
                last.then_inc(turned, 1)

            def x0_turn_waits(c):
                pe.wait_ge(base_in, (c + 1) * (16 * SH))
                wait(pe, x0c_ready, c * KT)
                wait(pe, g_out, (c - 1) * KT + U_X0T // NQ - 1)

            def x0_turn():
                for k in range(KT):
                    last = pe.transpose(x0_turned_e[:, k * M:(k + 1) * M], base[0:M, k * P:(k + 1) * P],
                                        ident[0:M, 0:M])
                last.then_inc(x0_turned, 1)

            def fold(c, j):
                pe.wait_ge(prod_done, c * NJ + j + 1)
                if j == 0:
                    wait(pe, x1l_done, 2 * c)
                    wait(pe, z1_done, c)
                b = prod_slot(j)
                pe.matmul(x_bank[:, :], w0_t[:, j * H:(j + 1) * H], prod[0:PB, b * CW:(b + 1) * CW],
                          start=(j == 0), stop=(j == NJ - 1)).then_inc(folded, 1)

            def unit(c, k, q, late):
                t = c * KT + k
                u = k * NQ + q
                if q == 0:
                    pe.wait_ge(x1l_done, 2 * c + (2 if k == KT - 1 else 1))
                wait(pe, *freed_by((u - NY) % NQ, c, (u - NY) // NQ, late))
                bank = y_bank[u % NY][:, :]
                hi, lo = x1_hi[:, k * P:(k + 1) * P], x1_lo[:, k * P:(k + 1) * P]
                s = slice(q * CW, (q + 1) * CW)
                pe.matmul(bank, hi, k1_lo[:, s], start=True, stop=False)
                pe.matmul(bank, hi, k1_hi[:, s], start=False, stop=False)
                pe.matmul(bank, lo, k1_hi[:, s], start=False, stop=True).then_inc(y_ready, 1)

            def g_matmul(t, k, copied):
                par = k % 2
                pe.wait_ge(x0c_ready, copied)
                pe.wait_ge(x2_ready, t + 1)
                pe.wait_ge(diag_ready, t + 1)
                wait(pe, g_out, t)
                pe.matmul(g_bank[:, 0:TB * M1], x2t[:, par * H:(par + 1) * H], diag[:, :],
                          start=True, stop=True).then_inc(g_done, 1)

            def dense_turn():
                pe.wait_ge(small_in, 16 * 4)
                pe.wait_ge(z1_done, NC)
                pe.wait_ge(turn_out, NBT * NG)
                pe.transpose(x_bank[:, 0:J1 + 2 * J2], rows[:, :], ident[0:J1 + 2 * J2, 0:J1 + 2 * J2])
                for t in range(NBT):
                    last = pe.transpose(e_bank[0:ND, t * P:(t + 1) * P], dense[:, t * ND:(t + 1) * ND], ident[:, :])
                last.then_inc(dense_done, 1)

            def h1_begin(j):
                pe.matmul(h1_bank[j][:, :], w1[:, j * P:(j + 1) * P], z1[:, :], start=True, stop=False)
                pe.matmul(h1_bank[j][:, :], w1d[:, j * P:(j + 1) * P], dense_t, start=False, stop=False)

            def chunk(c, late, prep=True, layer1=True):
                for u in range(KT * NQ):
                    k, q = divmod(u, NQ)
                    if not layer1 and u == U_DENSE:
                        dense_turn()
                    for n, u_turn, u_out in preps(c) if prep else ():
                        if u == u_turn:
                            turn(n)
                    if layer1:
                        if u == U_X0T - 1:
                            x0_turn_waits(c + 1)
                        if u == U_X0T:
                            x0_turn()
                        if u in U_FOLD:
                            fold(c + 1, U_FOLD.index(u))
                    if q == Q_G and not (k == 0 and isinstance(c, int) and c == 0):
                        g_matmul(c * KT + k - 1, (k - 1) % KT, c * KT + k + 2 if layer1 or k < KT - 1 else NT)
                    unit(c, k, q, late)

            for i in range(len(GROUPS)):
                setup_turn(i)
            for n in range(NG):
                turn(n)
            for j in range(NJ):
                if j == SH:
                    x0_turn_waits(0)
                fold(0, j)
                if j == SH:
                    x0_turn()
            pe.wait_ge(act_setup, len(GROUPS))
            pe.wait_ge(dve_setup, NQ)
            chunk(0, 0)
            chunk(1, 0)
            with pe.Fori(2, LATE) as c:
                chunk(c, 0)
            with pe.Fori(LATE, NC - NG) as c:
                chunk(c, 1)
            with pe.Fori(NC - NG, NC - 1) as c:
                chunk(c, 1, prep=False)
            chunk(NC - 1, 1, prep=False, layer1=False)
            pe.wait_ge(w_in, 16 * 2)
            pe.wait_ge(dense_out, 2)
            pe.wait_ge(z1_done, NC)
            for j in range(J1 - 2):
                h1_begin(j)
            g_matmul(NT - 1, KT - 1, NT)
            pe.wait_ge(a_unit, a_units(NC, 0, 1))
            pe.wait_ge(v_step, v_steps(NC, 0, 1))
            h1_begin(J1 - 2)
            h1_begin(J1 - 1)
            for m in range(M):
                if m % UM == 0:
                    pe.wait_ge(k2_lo_done, m // UM + 1)
                at_m = k2_slot(m // UM).start + m % UM * H
                hi, lo = (half[:, at_m:at_m + H] for half in (k1_hi, k1_lo))
                pe.wait_ge(g_hi_done, m + 1)
                pe.matmul(y_bank[0][:, :], lo, G_hi[m % NG3], start=(m == 0), stop=False)
                pe.matmul(y_bank[0][:, :], hi, G_hi[m % NG3], start=False, stop=False)
                pe.wait_ge(g_lo_done, m + 1)
                pe.matmul(y_bank[0][:, :], hi, G_lo[m % NG3], start=False, stop=(m == M - 1)).then_inc(z3_step, 1)
            for j in range(J1):
                pe.matmul(h1_bank[j][:, :], w1[:, N1 + j * P:N1 + (j + 1) * P], G[:, M, :], start=False, stop=False)
            pe.wait_ge(z3_out, 1)
            for j in range(J1):
                pe.matmul(h1_bank[j][:, :], w1[:, 2 * N1 + j * P:2 * N1 + (j + 1) * P], z3,
                          start=False, stop=True).then_inc(h1_done, 1)
            pe.wait_ge(w2_in, 16)
            for i in range(J2):
                for j in range(J1):
                    if i == 0:
                        pe.wait_ge(*((h1_act, j // 2 + 1) if j % 2 == 0 else (h1_dve, j // 2 + 1)))
                    last = pe.matmul(h2_bank[i][:, :], w2[:, j * N2 + i * P:j * N2 + (i + 1) * P],
                                     h1[:, j * B:(j + 1) * B], start=(j == 0), stop=(j == J1 - 1))
                last.then_inc(h2_done, 1)
            pe.wait_ge(h2_act, 1)
            pe.matmul(g_bank[0:1, 0:B], w3c[:, 0:1], h2[:, 0:B], start=True, stop=False)
            pe.wait_ge(h2_dve, 1)
            pe.matmul(g_bank[0:1, 0:B], w3c[:, 1:2], h2[:, B:2 * B], start=False, stop=True).then_inc(y_done, 1)


N_TABLES = 40
_INS = ["dense_ctx", "ids"] + [f"tbl_{i}" for i in range(N_TABLES)] + \
       ["W_top1", "b_top1", "W_top2", "b_top2", "W_top3", "L0_rec_k0", "L0_rec_k1", "L0_rec_k2"]


def kernel(**inputs):
    import numpy as _np
    import concourse.bacc as _bacc
    from concourse import mybir as _mybir
    from concourse.bass_utils import run_bass_kernel_spmd as _run

    nc = _bacc.Bacc("TRN2", target_bir_lowering=False, num_devices=1)
    arrays, aps = {}, {}
    for name in _INS:
        a = _np.ascontiguousarray(inputs[name])
        arrays[f"in_{name}_dram"] = a
        aps[name] = nc.dram_tensor(f"in_{name}_dram", a.shape, _mybir.dt.from_np(a.dtype), kind="ExternalInput").ap()
    out = nc.dram_tensor("out_0_dram", (aps["ids"].shape[0], 1), _mybir.dt.float32, kind="ExternalOutput").ap()
    cin_tower(nc, aps["dense_ctx"], aps["ids"], [aps[f"tbl_{i}"] for i in range(N_TABLES)],
              aps["W_top1"], aps["b_top1"], aps["W_top2"], aps["b_top2"], aps["W_top3"],
              aps["L0_rec_k0"], aps["L0_rec_k1"], aps["L0_rec_k2"], out)
    r = _run(nc, [arrays], core_ids=[0])
    return r.results[0]["out_0_dram"]
```
